# Optimizing a Trainium2 kernel written in Bass

```python
import numpy as np
import jax
import jax.numpy as jnp

def _softmax(x, axis=-1):
    return jax.nn.softmax(x, axis=axis)

def _gelu(x):
    return jax.nn.gelu(x, approximate=True)

def _silu(x):
    return jax.nn.silu(x)

def _sigmoid(x):
    return jax.nn.sigmoid(x)

def _layernorm(x, axis=-1, eps=1e-05):
    m = jnp.mean(x, axis=axis, keepdims=True)
    v = jnp.var(x, axis=axis, keepdims=True)
    return (x - m) / jnp.sqrt(v + eps)

def _scatter_add(tgt, idx, src, axis=0):
    return tgt.at[idx].add(src)

def _segment_sum(src, seg, n):
    return jax.ops.segment_sum(src, seg, n)
kernel_name = 'mk_adj_seq_d4_adj_r2_c7b231'

def setup_inputs(seed: int=0):
    np.random.seed(seed)
    _w = jnp.asarray

    def _rec_inputs():
        import jax
        import jax.numpy as jnp
        _gk = jax.random.key(seed)
        x = -0.0002928 + 1 * jax.random.normal(jax.random.fold_in(_gk, 1), (128, 128, 256), jnp.float32)
        _a = jax.random.bernoulli(jax.random.fold_in(_gk, 2), 0.03125, (128, 128, 128))
        _a = jnp.logical_or(_a, jnp.swapaxes(_a, -1, -2))
        _a = jnp.logical_or(_a, jnp.eye(128, dtype=bool))
        adj = _a.astype(jnp.int32)
        return (x, adj)
    x, adj = _rec_inputs()

    def _L0_gnn_setup():
        import jax, jax.numpy as jnp
        import numpy as np
        B, N, D, H = (4, 1024, 256, 8)
        HD = D // H
        EPS = 1e-05
        key = jax.random.key(seed)
        ks = jax.random.split(key, 12)
        x = jax.random.normal(ks[0], (B, N, D), dtype=jnp.float32)
        adj = jax.random.randint(ks[1], (B, N, N), 0, 2, dtype=jnp.int32)
        adj = jnp.maximum(adj, jnp.eye(N, dtype=jnp.int32)[None, :, :])
        s = 1.0 / np.sqrt(D)
        Wq = jax.random.uniform(ks[2], (D, D), jnp.float32, -s, s)
        bq = jnp.zeros((D,), jnp.float32)
        Wk = jax.random.uniform(ks[3], (D, D), jnp.float32, -s, s)
        bk = jnp.zeros((D,), jnp.float32)
        Wv = jax.random.uniform(ks[4], (D, D), jnp.float32, -s, s)
        bv = jnp.zeros((D,), jnp.float32)
        Wo = jax.random.uniform(ks[5], (D, D), jnp.float32, -s, s)
        bo = jnp.zeros((D,), jnp.float32)
        gamma = jnp.ones((D,), jnp.float32)
        beta = jnp.zeros((D,), jnp.float32)
        return {'x': x, 'adj': adj, 'Wq': Wq, 'bq': bq, 'Wk': Wk, 'bk': bk, 'Wv': Wv, 'bv': bv, 'Wo': Wo, 'bo': bo, 'gamma': gamma, 'beta': beta}
    _L0_gnn_all = _L0_gnn_setup()
    _L0_gnn_in = {k: v for k, v in _L0_gnn_all.items() if k in ('Wq', 'bq', 'Wk', 'bk', 'Wv', 'bv', 'Wo', 'bo', 'gamma', 'beta')}
    del _L0_gnn_all

    def _L1_gnn_setup():
        import jax, jax.numpy as jnp
        import numpy as np
        import math
        D = 256
        B, L = (8, 1024)
        EPS = 1e-05

        def layer_norm(y, gamma, beta):
            mu = jnp.mean(y, axis=-1, keepdims=True)
            var = jnp.mean(jnp.square(y - mu), axis=-1, keepdims=True)
            return (y - mu) * jax.lax.rsqrt(var + EPS) * gamma + beta
        key = jax.random.key(seed)
        ks = jax.random.split(key, 8)
        s = 1.0 / math.sqrt(D)
        x = jax.random.normal(ks[0], (B, L, D), dtype=jnp.float32)
        adj = jax.random.randint(ks[1], (B, L, L), 0, 2, dtype=jnp.int32)
        Wq = jax.random.normal(ks[2], (D, D), dtype=jnp.float32) * s
        Wk = jax.random.normal(ks[3], (D, D), dtype=jnp.float32) * s
        Wv = jax.random.normal(ks[4], (D, D), dtype=jnp.float32) * s
        Wo = jax.random.normal(ks[5], (D, D), dtype=jnp.float32) * s
        bo = jnp.zeros((D,), dtype=jnp.float32)
        gamma = jnp.ones((D,), dtype=jnp.float32)
        beta = jnp.zeros((D,), dtype=jnp.float32)
        return {'x': x, 'adj': adj, 'Wq': Wq, 'Wk': Wk, 'Wv': Wv, 'Wo': Wo, 'bo': bo, 'gamma': gamma, 'beta': beta}
    _L1_gnn_all = _L1_gnn_setup()
    _L1_gnn_in = {k: v for k, v in _L1_gnn_all.items() if k in ('Wq', 'Wk', 'Wv', 'Wo', 'bo', 'gamma', 'beta')}
    del _L1_gnn_all

    def _L2_gnn_setup():
        import jax, jax.numpy as jnp
        import numpy as np
        B, N, E, FF, L = (8, 1024, 256, 128, 2)
        LN_EPS = 1e-05
        SCALE = float(np.sqrt(FF))

        def layer_norm(x, g, b):
            m = jnp.mean(x, axis=-1, keepdims=True)
            v = jnp.mean(jnp.square(x - m), axis=-1, keepdims=True)
            return (x - m) * jax.lax.rsqrt(v + LN_EPS) * g + b
        key = jax.random.key(seed)
        ks = jax.random.split(key, 9)
        s = 0.02
        node_fts = jax.random.normal(ks[0], (B, N, E), jnp.float32)
        rel_edges = jax.random.randint(ks[1], (B, N, N), 0, 2, jnp.int32)
        Wq = jax.random.normal(ks[2], (L, FF, E), jnp.float32) * s
        bq = jnp.zeros((L, FF), jnp.float32)
        Wk = jax.random.normal(ks[3], (L, FF, E), jnp.float32) * s
        bk = jnp.zeros((L, FF), jnp.float32)
        Wc = jax.random.normal(ks[4], (L, E, E), jnp.float32) * s
        ln_g = jnp.ones((L, E), jnp.float32)
        ln_b = jnp.zeros((L, E), jnp.float32)
        return {'node_fts': node_fts, 'rel_edges': rel_edges, 'Wq': Wq, 'bq': bq, 'Wk': Wk, 'bk': bk, 'Wc': Wc, 'ln_g': ln_g, 'ln_b': ln_b}
    _L2_gnn_all = _L2_gnn_setup()
    _L2_gnn_in = {k: v for k, v in _L2_gnn_all.items() if k in ('Wq', 'bq', 'Wk', 'bk', 'Wc', 'ln_g', 'ln_b')}
    del _L2_gnn_all

    def _L3_gnn_setup():
        import jax, jax.numpy as jnp
        import numpy as np
        B, N, E, FF, L = (8, 1024, 256, 128, 2)
        LN_EPS = 1e-05
        SCALE = float(np.sqrt(FF))

        def layer_norm(x, g, b):
            m = jnp.mean(x, axis=-1, keepdims=True)
            v = jnp.mean(jnp.square(x - m), axis=-1, keepdims=True)
            return (x - m) * jax.lax.rsqrt(v + LN_EPS) * g + b
        key = jax.random.key(seed)
        ks = jax.random.split(key, 9)
        s = 0.02
        node_fts = jax.random.normal(ks[0], (B, N, E), jnp.float32)
        rel_edges = jax.random.randint(ks[1], (B, N, N), 0, 2, jnp.int32)
        Wq = jax.random.normal(ks[2], (L, FF, E), jnp.float32) * s
        bq = jnp.zeros((L, FF), jnp.float32)
        Wk = jax.random.normal(ks[3], (L, FF, E), jnp.float32) * s
        bk = jnp.zeros((L, FF), jnp.float32)
        Wc = jax.random.normal(ks[4], (L, E, E), jnp.float32) * s
        ln_g = jnp.ones((L, E), jnp.float32)
        ln_b = jnp.zeros((L, E), jnp.float32)
        return {'node_fts': node_fts, 'rel_edges': rel_edges, 'Wq': Wq, 'bq': bq, 'Wk': Wk, 'bk': bk, 'Wc': Wc, 'ln_g': ln_g, 'ln_b': ln_b}
    _L3_gnn_all = _L3_gnn_setup()
    _L3_gnn_in = {k: v for k, v in _L3_gnn_all.items() if k in ('Wq', 'bq', 'Wk', 'bk', 'Wc', 'ln_g', 'ln_b')}
    del _L3_gnn_all
    return {'x': x, 'adj': adj, 'L0_gnn_Wq': _L0_gnn_in['Wq'], 'L0_gnn_bq': _L0_gnn_in['bq'], 'L0_gnn_Wk': _L0_gnn_in['Wk'], 'L0_gnn_bk': _L0_gnn_in['bk'], 'L0_gnn_Wv': _L0_gnn_in['Wv'], 'L0_gnn_bv': _L0_gnn_in['bv'], 'L0_gnn_Wo': _L0_gnn_in['Wo'], 'L0_gnn_bo': _L0_gnn_in['bo'], 'L0_gnn_gamma': _L0_gnn_in['gamma'], 'L0_gnn_beta': _L0_gnn_in['beta'], 'L1_gnn_Wq': _L1_gnn_in['Wq'], 'L1_gnn_Wk': _L1_gnn_in['Wk'], 'L1_gnn_Wv': _L1_gnn_in['Wv'], 'L1_gnn_Wo': _L1_gnn_in['Wo'], 'L1_gnn_bo': _L1_gnn_in['bo'], 'L1_gnn_gamma': _L1_gnn_in['gamma'], 'L1_gnn_beta': _L1_gnn_in['beta'], 'L2_gnn_Wq': _L2_gnn_in['Wq'], 'L2_gnn_bq': _L2_gnn_in['bq'], 'L2_gnn_Wk': _L2_gnn_in['Wk'], 'L2_gnn_bk': _L2_gnn_in['bk'], 'L2_gnn_Wc': _L2_gnn_in['Wc'], 'L2_gnn_ln_g': _L2_gnn_in['ln_g'], 'L2_gnn_ln_b': _L2_gnn_in['ln_b'], 'L3_gnn_Wq': _L3_gnn_in['Wq'], 'L3_gnn_bq': _L3_gnn_in['bq'], 'L3_gnn_Wk': _L3_gnn_in['Wk'], 'L3_gnn_bk': _L3_gnn_in['bk'], 'L3_gnn_Wc': _L3_gnn_in['Wc'], 'L3_gnn_ln_g': _L3_gnn_in['ln_g'], 'L3_gnn_ln_b': _L3_gnn_in['ln_b']}

def reference(x, adj, L0_gnn_Wq, L0_gnn_bq, L0_gnn_Wk, L0_gnn_bk, L0_gnn_Wv, L0_gnn_bv, L0_gnn_Wo, L0_gnn_bo, L0_gnn_gamma, L0_gnn_beta, L1_gnn_Wq, L1_gnn_Wk, L1_gnn_Wv, L1_gnn_Wo, L1_gnn_bo, L1_gnn_gamma, L1_gnn_beta, L2_gnn_Wq, L2_gnn_bq, L2_gnn_Wk, L2_gnn_bk, L2_gnn_Wc, L2_gnn_ln_g, L2_gnn_ln_b, L3_gnn_Wq, L3_gnn_bq, L3_gnn_Wk, L3_gnn_bk, L3_gnn_Wc, L3_gnn_ln_g, L3_gnn_ln_b):
    import jax
    import jax.numpy as jnp

    def _L0_gnn_ref(x, adj, Wq, bq, Wk, bk, Wv, bv, Wo, bo, gamma, beta):
        import jax, jax.numpy as jnp
        import numpy as np
        B, N, D, H = (4, 1024, 256, 8)
        HD = D // H
        EPS = 1e-05
        b, n, d = x.shape
        scale = 1.0 / np.sqrt(HD).astype(np.float32)
        q = (x @ Wq + bq).reshape(b, n, H, HD)
        k = (x @ Wk + bk).reshape(b, n, H, HD)
        v = (x @ Wv + bv).reshape(b, n, H, HD)
        scores = jnp.einsum('bnhd,bmhd->bhnm', q, k) * scale
        mask = (adj == 0)[:, None, :, :]
        scores = jnp.where(mask, jnp.float32(-jnp.inf), scores)
        attn = jax.nn.softmax(scores, axis=-1)
        h = jnp.einsum('bhnm,bmhd->bnhd', attn, v).reshape(b, n, d)
        h = h @ Wo + bo
        y = h + x
        mu = jnp.mean(y, axis=-1, keepdims=True)
        var = jnp.mean(jnp.square(y - mu), axis=-1, keepdims=True)
        return (y - mu) * jax.lax.rsqrt(var + EPS) * gamma + beta

    def _L1_gnn_ref(x, adj, Wq, Wk, Wv, Wo, bo, gamma, beta):
        import jax, jax.numpy as jnp
        import numpy as np
        import math
        D = 256
        B, L = (8, 1024)
        EPS = 1e-05

        def layer_norm(y, gamma, beta):
            mu = jnp.mean(y, axis=-1, keepdims=True)
            var = jnp.mean(jnp.square(y - mu), axis=-1, keepdims=True)
            return (y - mu) * jax.lax.rsqrt(var + EPS) * gamma + beta
        d_out = Wq.shape[1]
        scale = 1.0 / math.sqrt(d_out)
        Q = x @ Wq
        K = x @ Wk
        V = x @ Wv
        sc = jnp.einsum('bld,bmd->blm', Q, K) * scale
        mask = adj == 0
        sc = jnp.where(mask, -jnp.inf, sc)
        all_inf = jnp.all(mask, axis=-1, keepdims=True)
        sc = jnp.where(all_inf, 0.0, sc)
        w = jax.nn.softmax(sc, axis=-1)
        out = jnp.einsum('blm,bmd->bld', w, V)
        y = x + out @ Wo + bo
        return layer_norm(y, gamma, beta)

    def _L2_gnn_ref(node_fts, rel_edges, Wq, bq, Wk, bk, Wc, ln_g, ln_b):
        import jax, jax.numpy as jnp
        import numpy as np
        B, N, E, FF, L = (8, 1024, 256, 128, 2)
        LN_EPS = 1e-05
        SCALE = float(np.sqrt(FF))

        def layer_norm(x, g, b):
            m = jnp.mean(x, axis=-1, keepdims=True)
            v = jnp.mean(jnp.square(x - m), axis=-1, keepdims=True)
            return (x - m) * jax.lax.rsqrt(v + LN_EPS) * g + b
        x = node_fts
        mask = rel_edges == 0
        for k in range(L):
            q = jnp.einsum('bnd,fd->bnf', x, Wq[k]) + bq[k]
            kk = jnp.einsum('bnd,fd->bnf', x, Wk[k]) + bk[k]
            scores = jnp.einsum('bof,bif->boi', q, kk) / SCALE
            scores = jnp.where(mask, -10000000000.0, scores)
            attn = jax.nn.softmax(scores, axis=2)
            attn = jnp.where(mask, 0.0, attn)
            ctx = jnp.einsum('boi,bid->bod', attn, x)
            ctx = jnp.einsum('bnd,ed->bne', ctx, Wc[k])
            x = layer_norm(x + ctx, ln_g[k], ln_b[k])
        return x

    def _L3_gnn_ref(node_fts, rel_edges, Wq, bq, Wk, bk, Wc, ln_g, ln_b):
        import jax, jax.numpy as jnp
        import numpy as np
        B, N, E, FF, L = (8, 1024, 256, 128, 2)
        LN_EPS = 1e-05
        SCALE = float(np.sqrt(FF))

        def layer_norm(x, g, b):
            m = jnp.mean(x, axis=-1, keepdims=True)
            v = jnp.mean(jnp.square(x - m), axis=-1, keepdims=True)
            return (x - m) * jax.lax.rsqrt(v + LN_EPS) * g + b
        x = node_fts
        mask = rel_edges == 0
        for k in range(L):
            q = jnp.einsum('bnd,fd->bnf', x, Wq[k]) + bq[k]
            kk = jnp.einsum('bnd,fd->bnf', x, Wk[k]) + bk[k]
            scores = jnp.einsum('bof,bif->boi', q, kk) / SCALE
            scores = jnp.where(mask, -10000000000.0, scores)
            attn = jax.nn.softmax(scores, axis=2)
            attn = jnp.where(mask, 0.0, attn)
            ctx = jnp.einsum('boi,bid->bod', attn, x)
            ctx = jnp.einsum('bnd,ed->bne', ctx, Wc[k])
            x = layer_norm(x + ctx, ln_g[k], ln_b[k])
        return x
    x = _L0_gnn_ref(x, adj, L0_gnn_Wq, L0_gnn_bq, L0_gnn_Wk, L0_gnn_bk, L0_gnn_Wv, L0_gnn_bv, L0_gnn_Wo, L0_gnn_bo, L0_gnn_gamma, L0_gnn_beta)
    x = _L1_gnn_ref(x, adj, L1_gnn_Wq, L1_gnn_Wk, L1_gnn_Wv, L1_gnn_Wo, L1_gnn_bo, L1_gnn_gamma, L1_gnn_beta)
    x = _L2_gnn_ref(x, adj, L2_gnn_Wq, L2_gnn_bq, L2_gnn_Wk, L2_gnn_bk, L2_gnn_Wc, L2_gnn_ln_g, L2_gnn_ln_b)
    x = _L3_gnn_ref(x, adj, L3_gnn_Wq, L3_gnn_bq, L3_gnn_Wk, L3_gnn_bk, L3_gnn_Wc, L3_gnn_ln_g, L3_gnn_ln_b)
    return x

_drawn_inputs = setup_inputs


def setup_inputs(seed=0):
    import zlib

    import numpy as np

    out = dict(_drawn_inputs(seed))
    spreads = {'L0_gnn_bq': (0.0, 0.8),
     'L0_gnn_bk': (0.0, 0.8),
     'L0_gnn_bv': (0.0, 0.1),
     'L0_gnn_bo': (0.0, 0.1),
     'L0_gnn_gamma': (1.0, 0.2),
     'L0_gnn_beta': (0.0, 0.1),
     'L1_gnn_bo': (0.0, 0.1),
     'L1_gnn_gamma': (1.0, 0.2),
     'L1_gnn_beta': (0.0, 0.1),
     'L2_gnn_bq': (0.0, 0.8),
     'L2_gnn_bk': (0.0, 0.8),
     'L2_gnn_ln_g': (1.0, 0.2),
     'L2_gnn_ln_b': (0.0, 0.1),
     'L3_gnn_bq': (0.0, 0.8),
     'L3_gnn_bk': (0.0, 0.8),
     'L3_gnn_ln_g': (1.0, 0.2),
     'L3_gnn_ln_b': (0.0, 0.1)}
    factors = {'L2_gnn_Wq': 3.894, 'L2_gnn_Wk': 3.73, 'L3_gnn_Wq': 3.884, 'L3_gnn_Wk': 3.736}
    for name, (base, spread) in spreads.items():
        noise = np.random.default_rng([zlib.crc32(name.encode()), seed]).standard_normal(out[name].shape)
        drawn = base * np.exp(spread * noise) if base else spread * noise
        out[name] = jnp.asarray(drawn.astype(out[name].dtype))
    for name, factor in factors.items():
        out[name] = (out[name] * factor).astype(out[name].dtype)
    return out
```

```python
from contextlib import ExitStack

import concourse.bass as bass
from concourse import mybir

F32 = mybir.dt.float32
BF16 = mybir.dt.bfloat16
I32 = mybir.dt.int32
ALU = mybir.AluOpType
ACT = mybir.ActivationFunctionType
AX_X = mybir.AxisListType.X

GRAPHS, N, D = 128, 128, 256
P = 128
KD = D // P
G = 2
S = 4
PASSES = GRAPHS // (G * S)
HEADS = 8
HD = D // HEADS
QUAD = P // HD
LAYERS = 6
TILES = HEADS + LAYERS - 1
EPS = 1e-5
MASKED = -(2.0**100)
SCALE = [HD**-0.5, D**-0.5] + [P**-0.5] * 4

WEIGHTS = {}
_at = 0
for _name, _width in (
    [("wq0", D), ("wk0", D), ("wv0", D), ("wo0", D), ("wqT1", D), ("wkT1", D), ("wvT1", D), ("wo1", D)]
    + [(f"{m}{layer}", w) for layer in range(2, LAYERS) for m, w in (("wqT", P), ("wkT", P), ("wcT", D))]
):
    WEIGHTS[_name] = (_at, _width)
    _at += KD * _width
WEIGHT_COLUMNS = _at
ROWS = ["bv0", "bo0", "bo1"] + [f"{m}{layer}" for layer in range(LAYERS) for m in ("gamma", "beta")]
COLUMNS = {"bq0": 0, "bk0": KD} | {f"{m}{layer}": 2 * KD + 2 * (layer - 2) + n
                                   for layer in range(2, LAYERS) for n, m in enumerate(("bq", "bk"))}
COLUMN_COUNT = 2 * KD + 2 * (LAYERS - 2)


def tile_of(layer, head=0):
    return head if layer == 0 else HEADS + layer - 1


def gnn_stack(nc: bass.Bass, x_in, xT_in, adj_in, w_in, rows_in, cols_in, eye_in, out):
    ctx = ExitStack()

    def sb(name, shape, dtype=F32):
        return ctx.enter_context(nc.sbuf_tensor(name, [P] + shape, dtype))

    def sem(name):
        return ctx.enter_context(nc.semaphore(name))

    def sems(name):
        return [sem(f"{name}_{s}") for s in range(S)]

    with ctx:
        weights = sb("weights", [WEIGHT_COLUMNS])
        rows = sb("rows", [len(ROWS), D])
        cols = sb("cols", [COLUMN_COUNT])
        eye = sb("eye", [P])
        eye16 = sb("eye16", [P], BF16)
        score_weights = sb("score_weights", [KD, D])
        value_weights = sb("value_weights", [KD, D])
        x0 = sb("x0", [S, G, D])
        x0T = sb("x0T", [S, KD, G, N])
        adj = sb("adj", [S, G, N], I32)
        x_out = sb("x_out", [S, G, D])
        mask = sb("mask", [S, G, N], BF16)
        x = sb("x", [S, G, D])
        residual = sb("residual", [S, G, D])
        xT = sb("xT", [S, KD, G, N])
        qT = sb("qT", [S, KD, G, N])
        kT = sb("kT", [S, KD, G, N])
        v = sb("v", [S, G, D])
        probs = sb("probs", [S, G, N])
        probsT = sb("probsT", [S, G, N])
        headsT = sb("headsT", [S, HEADS // QUAD, G, N])
        y = sb("y", [S, G, D])
        z = sb("z", [S, G, D])
        zg = sb("zg", [S, G, D])
        negmax = sb("negmax", [S, G])
        valid = sb("valid", [S, G])
        total = sb("total", [S, G])
        rtotal = sb("rtotal", [S, G])
        bn = sb("bn", [S, G, 6])
        mv = sb("mv", [S, G, 2])
        log_var = sb("log_var", [S, G])
        rough = sb("rough", [S, G])
        step_a = sb("step_a", [S, G])
        step_b = sb("step_b", [S, G])
        rstd = sb("rstd", [S, G])
        shift = sb("shift", [S, G])
        eps = sb("eps", [1])

        bank = [[ctx.enter_context(nc.psum_tensor(f"bank{b}_{s}", [P, 512], F32)) for s in range(S)] for b in "AB"]
        A, B = bank

        consts_loaded = sem("consts_loaded")
        loaded = sem("loaded")
        go = sem("go")
        go_cleared = sem("go_cleared")
        stored = sem("stored")
        x_out_free = sem("x_out_free")
        eye16_ready = sem("eye16_ready")
        fused_in_psum = sem("fused_in_psum")
        fused_ready = sem("fused_ready")
        dve_step = sem("dve_step")
        mask_ready = sems("mask_ready")
        residual_ready = sems("residual_ready")
        valid_ready = sems("valid_ready")
        xT_in_psum = sems("xT_in_psum")
        xT_ready = sems("xT_ready")
        qk_in_psum = sems("qk_in_psum")
        qk_ready = sems("qk_ready")
        k0_ready = sems("k0_ready")
        v_in_psum = sems("v_in_psum")
        v_ready = sems("v_ready")
        scores_in_psum = sems("scores_in_psum")
        negmax_ready = sems("negmax_ready")
        exp_ready = sems("exp_ready")
        probs_ready = sems("probs_ready")
        probsT_in_psum = sems("probsT_in_psum")
        probsT_ready = sems("probsT_ready")
        headsT_in_psum = sems("headsT_in_psum")
        headsT_ready = sems("headsT_ready")
        context_in_psum = sems("context_in_psum")
        stats_ready = sems("stats_ready")
        log_ready = sems("log_ready")
        rough_ready = sems("rough_ready")
        rstd_ready = sems("rstd_ready")
        z_ready = sems("z_ready")
        zg_ready = sems("zg_ready")
        x_ready = sems("x_ready")

        per_pass = [dve_step] + [q for group in (
            mask_ready, residual_ready, valid_ready, xT_in_psum, xT_ready, qk_in_psum, qk_ready, k0_ready, v_in_psum,
            v_ready, scores_in_psum, negmax_ready, exp_ready, probs_ready, probsT_in_psum, probsT_ready,
            headsT_in_psum, headsT_ready, context_in_psum, stats_ready, log_ready, rough_ready, rstd_ready,
            z_ready, zg_ready, x_ready) for q in group] + [x_out_free, go_cleared]

        def w(name, kd, lo=0, hi=None):
            at, width = WEIGHTS[name]
            return weights[:, at + kd * width + lo:at + kd * width + (width if hi is None else hi)]

        def row(name):
            return rows[:, ROWS.index(name), :]

        def row_of_each(name):
            return rows[:, ROWS.index(name):ROWS.index(name) + 1, :].to_broadcast([P, G, D])

        def col(name, ft=0):
            return cols[:, COLUMNS[name] + ft:COLUMNS[name] + ft + 1]

        def by_graph(psum, width):
            return psum[:, 0:G * width].rearrange("p (g n) -> p g n", g=G)

        def flat(t):
            return t.rearrange("p g n -> p (g n)")

        chain = [(layer, s) for layer in range(1, LAYERS) for s in range(S)]
        first = [(0, s) for s in range(S)]
        slots = range(-2, len(chain) + 2)

        def item(i):
            if -2 <= i + 2 and i < len(chain):
                return chain[i] if i >= 0 else None
            return None

        def normalised(i):
            k = i - 2 + S
            return (first + chain)[k] if 0 <= k < S + len(chain) else None

        head_steps = range(HEADS * S + 2 * S)

        def head_of(j):
            return (j // S, j % S) if 0 <= j < HEADS * S else None

        block = ctx.enter_context(nc.Block())

        @block.sync
        def _(sp):
            sp.dma_start(weights[:, :], w_in).then_inc(consts_loaded, 16)
            sp.dma_start(rows[:, :, :], rows_in.partition_broadcast(P)).then_inc(consts_loaded, 16)
            sp.dma_start(cols[:, :], cols_in).then_inc(consts_loaded, 16)
            sp.dma_start(eye[:, :], eye_in).then_inc(consts_loaded, 16)
            sp.dma_start(x0[:, :, :, :], x_in[0]).then_inc(loaded, 16)
            sp.dma_start(x0T[:, :, :, :, :], xT_in[0]).then_inc(loaded, 16)
            sp.dma_start(adj[:, :, :, :], adj_in[0]).then_inc(loaded, 16)
            sp.sem_inc(stored, 16 * S)
            sp.wait_ge(consts_loaded, 64)
            sp.wait_ge(fused_ready, 4)
            with sp.Fori(0, PASSES) as i:
                sp.wait_ge(loaded, 48)
                sp.sem_clear(loaded)
                sp.sem_inc(go, 1)
                sp.wait_ge(stored, 16 * S)
                sp.sem_clear(stored)
                sp.sem_inc(x_out_free, 1)
                sp.wait_ge(v_ready[S - 1], 1)
                sp.wait_ge(k0_ready[S - 1], 1)
                sp.wait_ge(residual_ready[S - 1], 1)
                sp.nop(nofuse=True)
                sp.sem_clear(go)
                sp.sem_inc(go_cleared, 1)
                ahead = sp.snap((i + 1) % PASSES)
                sp.dma_start(x0[:, :, :, :], x_in[ahead]).then_inc(loaded, 16)
                sp.dma_start(x0T[:, :, :, :, :], xT_in[ahead]).then_inc(loaded, 16)
                sp.dma_start(adj[:, :, :, :], adj_in[ahead]).then_inc(loaded, 16)
                for s in range(S):
                    sp.wait_ge(x_ready[s], LAYERS)
                    sp.dma_start(out[i][:, s], x_out[:, s]).then_inc(stored, 16)
                for q in per_pass:
                    sp.sem_clear(q)
            sp.wait_ge(loaded, 48)
            sp.wait_ge(stored, 16 * S)

        @block.tensor
        def _(pe):
            pe.wait_ge(consts_loaded, 64)
            pe.wait_ge(eye16_ready, 1)
            for b, (left, right) in enumerate((("wqT1", "wkT1"), ("wvT1", "wo1"))):
                for ft in range(KD):
                    for kd in range(KD):
                        mm = pe.matmul(bank[b][ft][:, 0:D], w(left, kd, ft * P, ft * P + P), w(right, kd),
                                       start=kd == 0, stop=kd == KD - 1)
                    mm.then_inc(fused_in_psum, 1)
            pe.wait_ge(fused_ready, 4)

            def project(psum, s, source, parts):
                for n, (name, lo) in enumerate(parts):
                    for kd in range(KD):
                        lhs = w(name, kd, lo, lo + P) if name else score_weights[:, kd, lo:lo + P]
                        mm = pe.matmul(psum[:, n * G * N:(n + 1) * G * N], lhs, flat(source[:, s, kd]),
                                       start=kd == 0, stop=kd == KD - 1)
                return mm

            def values(psum, s, source, weight):
                for g in range(G):
                    for kd in range(KD):
                        mm = pe.matmul(psum[:, g * D:(g + 1) * D], source[:, s, kd, g], weight(kd),
                                       start=kd == 0, stop=kd == KD - 1)
                return mm

            def masked(s):
                pe.matmul(B[s][:, 0:G * N], eye16[:, :], flat(mask[:, s]), start=True, stop=False)

            def transpose_probs(s, layer, head=0):
                pe.wait_ge(probs_ready[s] if layer == 0 else exp_ready[s], tile_of(layer, head) + 1)
                for g in range(G):
                    t = pe.transpose(A[s][:, g * N:(g + 1) * N], probs[:, s, g], eye[:, :])
                t.then_inc(probsT_in_psum[s], 1)

            with pe.Fori(0, PASSES):
                pe.wait_ge(go, 1)
                pe.nop(nofuse=True)
                for s in range(S):
                    project(A[s], s, x0T, [("wq0", 0), ("wq0", P)]).then_inc(qk_in_psum[s], 1)
                    project(B[s], s, x0T, [("wk0", 0), ("wk0", P)]).then_inc(qk_in_psum[s], 1)
                    pe.wait_ge(qk_ready[s], 1)
                    values(A[s], s, x0T, lambda kd: w("wv0", kd)).then_inc(v_in_psum[s], 1)
                for j in head_steps:
                    if now := head_of(j - 2 * S):
                        head, s = now
                        pe.wait_ge(probsT_ready[s], head + 1)
                        r = head % QUAD * HD
                        for g in range(G):
                            mm = pe.matmul(A[s][r:r + HD, (G + g) * N:(G + g + 1) * N],
                                           v[:, s, g, head * HD:(head + 1) * HD], probsT[:, s, g],
                                           start=True, stop=True, tile_position=(0, r))
                        if head % QUAD == QUAD - 1:
                            mm.then_inc(headsT_in_psum[s], 1)
                    if now := head_of(j):
                        head, s = now
                        if head == 0:
                            pe.wait_ge(k0_ready[s], 1)
                            pe.wait_ge(mask_ready[s], 1)
                        else:
                            pe.wait_ge(exp_ready[s], head)
                        masked(s)
                        r = head % QUAD * HD
                        for g in range(G):
                            mm = pe.matmul(B[s][:, g * N:(g + 1) * N], qT[r:r + HD, s, head // QUAD, g],
                                           kT[r:r + HD, s, head // QUAD, g], start=False, stop=g == G - 1)
                        mm.then_inc(scores_in_psum[s], 1)
                    if now := head_of(j - S):
                        head, s = now
                        if head == 0:
                            pe.wait_ge(v_ready[s], 1)
                        if head == QUAD:
                            pe.wait_ge(headsT_ready[s], 1)
                        transpose_probs(s, 0, head)
                for s in range(S):
                    pe.wait_ge(headsT_ready[s], 2)
                    for g in range(G):
                        for kd in range(KD):
                            mm = pe.matmul(B[s][:, g * D:(g + 1) * D], headsT[:, s, kd, g], w("wo0", kd),
                                           start=kd == 0, stop=kd == KD - 1)
                    mm.then_inc(context_in_psum[s], 1)

                pe.wait_ge(go_cleared, 1)
                pe.nop(nofuse=True)
                for i in slots:
                    if now := item(i):
                        layer, s = now
                        pe.wait_ge(x_ready[s], layer)
                        for kd in range(KD):
                            for g in range(G):
                                t = pe.transpose(A[s][:, (kd * G + g) * N:(kd * G + g + 1) * N],
                                                 x[:, s, g, kd * P:(kd + 1) * P], eye[:, :])
                        t.then_inc(xT_in_psum[s], 1)
                    if now := item(i - 1):
                        layer, s = now
                        pe.wait_ge(qk_ready[s], layer + 1)
                        masked(s)
                        parts = range(KD) if layer == 1 else range(1)
                        for g in range(G):
                            for kd in parts:
                                keys = xT[:, s, kd, g] if layer == 1 else kT[:, s, 0, g]
                                mm = pe.matmul(B[s][:, g * N:(g + 1) * N], qT[:, s, kd, g], keys,
                                               start=False, stop=g == G - 1 and kd == parts[-1])
                        mm.then_inc(scores_in_psum[s], 1)
                    if now := item(i - 2):
                        layer, s = now
                        pe.wait_ge(probsT_ready[s], tile_of(layer) + 1)
                        for g in range(G):
                            mm = pe.matmul(B[s][:, g * D:(g + 1) * D], probsT[:, s, g], v[:, s, g],
                                           start=True, stop=True)
                        mm.then_inc(context_in_psum[s], 1)
                    if now := item(i):
                        layer, s = now
                        pe.wait_ge(xT_ready[s], layer)
                        parts = [("", 0), ("", P)] if layer == 1 else [(f"wqT{layer}", 0), (f"wkT{layer}", 0)]
                        project(B[s], s, xT, parts).then_inc(qk_in_psum[s], 1)
                    if now := item(i - 1):
                        layer, s = now
                        pe.wait_ge(v_ready[s], layer + 1)
                        transpose_probs(s, layer)
                    if now := item(i):
                        layer, s = now
                        weight = (lambda kd: value_weights[:, kd]) if layer == 1 else (
                            lambda kd: w(f"wcT{layer}", kd))
                        values(A[s], s, xT, weight).then_inc(v_in_psum[s], 1)

        @block.scalar
        def _(act):
            act.preload_act_table_set("natural_log_exp_and_others")
            act.wait_ge(eye16_ready, 1)
            for n in range(2):
                act.wait_ge(fused_in_psum, n + 1)
                act.copy(score_weights[:, n], A[n][:, 0:D]).then_inc(fused_ready, 1)

            def softmax(s, layer, head=0):
                act.wait_ge(negmax_ready[s], tile_of(layer, head) + 1)
                if layer == 0 and head > 0:
                    act.wait_ge(probsT_in_psum[s], head)
                for g in range(G):
                    e = act.activation(probs[:, s, g], B[s][:, g * N:(g + 1) * N], ACT.Exp,
                                       bias=negmax[:, s, g:g + 1], accum_out=total[:, s, g:g + 1])
                e.then_inc(exp_ready[s], 1)

            def move_probsT(s, layer, head=0):
                act.wait_ge(probsT_in_psum[s], tile_of(layer, head) + 1)
                act.copy(flat(probsT[:, s]), A[s][:, 0:G * N]).then_inc(probsT_ready[s], 1)

            with act.Fori(0, PASSES):
                act.wait_ge(go, 1)
                act.nop(nofuse=True)
                for s in range(S):
                    act.wait_ge(qk_in_psum[s], 2)
                    for ft in range(KD):
                        m = act.activation(flat(kT[:, s, ft]), B[s][:, ft * G * N:(ft + 1) * G * N], ACT.Identity,
                                           bias=col("bk0", ft))
                    m.then_inc(k0_ready[s], 1)
                for j in head_steps:
                    if now := head_of(j):
                        head, s = now
                        softmax(s, 0, head)
                    if now := head_of(j - S):
                        head, s = now
                        move_probsT(s, 0, head)
                act.wait_ge(go_cleared, 1)
                act.nop(nofuse=True)
                for i in slots:
                    if now := item(i):
                        layer, s = now
                        act.wait_ge(xT_in_psum[s], layer)
                        act.copy(xT[:, s].rearrange("p k g n -> p (k g n)"), A[s][:, :]).then_inc(xT_ready[s], 1)
                    if now := item(i - 1):
                        layer, s = now
                        softmax(s, layer)
                    if now := item(i - 1):
                        layer, s = now
                        move_probsT(s, layer)
                    if now := normalised(i):
                        layer, s = now
                        act.wait_ge(stats_ready[s], layer + 1)
                        act.activation(log_var[:, s], mv[:, s, :, 1], ACT.Ln,
                                       bias=eps[:, 0:1]).then_inc(log_ready[s], 1)
                        act.wait_ge(log_ready[s], layer + 1)
                        act.activation(rough[:, s], log_var[:, s], ACT.Exp, scale=-0.5).then_inc(rough_ready[s], 1)
                        act.wait_ge(rstd_ready[s], layer + 1)
                        for g in range(G):
                            m = act.activation(z[:, s, g], y[:, s, g], ACT.Identity, bias=shift[:, s, g:g + 1],
                                               scale=rstd[:, s, g:g + 1])
                        m.then_inc(z_ready[s], 1)
                    if now := item(i):
                        layer, s = now
                        act.wait_ge(v_in_psum[s], layer + 1)
                        act.copy(flat(v[:, s]), A[s][:, :]).then_inc(v_ready[s], 1)

        @block.vector
        def _(dve):
            dve.wait_ge(consts_loaded, 64)
            dve.memset(eps[:, :], EPS)
            dve.tensor_copy(eye16[:, :], eye[:, :]).then_inc(eye16_ready, 1)
            for n in range(2):
                dve.wait_ge(fused_in_psum, n + 3)
                dve.tensor_copy(value_weights[:, n], B[n][:, 0:D]).then_inc(fused_ready, 1)
            steps = [0]

            def settle(instruction):
                steps[0] += 1
                instruction.then_inc(dve_step, 1)
                dve.wait_ge(dve_step, steps[0])

            def row_max(s, layer, head=0):
                dve.wait_ge(scores_in_psum[s], tile_of(layer, head) + 1)
                dve.tensor_reduce(negmax[:, s], by_graph(B[s], N), AX_X, ALU.max,
                                  negate=True).then_inc(negmax_ready[s], 1)

            with dve.Fori(0, PASSES):
                steps[0] = 0
                dve.wait_ge(go, 1)
                dve.nop(nofuse=True)
                for s in range(S):
                    dve.tensor_scalar(mask[:, s], adj[:, s], 0.0, MASKED, ALU.is_equal,
                                      ALU.mult).then_inc(mask_ready[s], 1)
                for s in range(S):
                    dve.wait_ge(qk_in_psum[s], 1)
                    for ft in range(KD):
                        m = dve.tensor_scalar(flat(qT[:, s, ft]), A[s][:, ft * G * N:(ft + 1) * G * N],
                                              col("bq0", ft), SCALE[0], ALU.add, ALU.mult)
                    m.then_inc(qk_ready[s], 1)
                    dve.wait_ge(v_in_psum[s], 1)
                    dve.tensor_tensor(v[:, s], by_graph(A[s], D), row_of_each("bv0"),
                                      ALU.add).then_inc(v_ready[s], 1)
                for j in head_steps:
                    if now := head_of(j):
                        head, s = now
                        row_max(s, 0, head)
                        if head == 0:
                            dve.wait_ge(negmax_ready[s], 1)
                            dve.tensor_scalar(valid[:, s], negmax[:, s], -0.5 * MASKED, None,
                                              ALU.is_lt).then_inc(valid_ready[s], 1)
                    if now := head_of(j - 2):
                        head, s = now
                        dve.wait_ge(exp_ready[s], head + 1)
                        dve.wait_ge(valid_ready[s], 1)
                        settle(dve.tensor_tensor(rtotal[:, s], total[:, s], valid[:, s], ALU.mult))
                        settle(dve.reciprocal(rtotal[:, s], rtotal[:, s]))
                        for g in range(G):
                            m = dve.tensor_scalar(probs[:, s, g], probs[:, s, g], rtotal[:, s, g:g + 1], None,
                                                  ALU.mult)
                        m.then_inc(probs_ready[s], 1)
                    if (now := head_of(j - 2 * S)) and now[0] % QUAD == QUAD - 1:
                        head, s = now
                        dve.wait_ge(headsT_in_psum[s], head // QUAD + 1)
                        dve.tensor_copy(flat(headsT[:, s, head // QUAD]),
                                        A[s][:, G * N:2 * G * N]).then_inc(headsT_ready[s], 1)
                dve.wait_ge(go_cleared, 1)
                dve.nop(nofuse=True)
                for i in slots:
                    if now := item(i - 1):
                        layer, s = now
                        row_max(s, layer)
                    if now := normalised(i):
                        layer, s = now
                        if layer > 0:
                            dve.wait_ge(exp_ready[s], tile_of(layer) + 1)
                            settle(dve.reciprocal(rtotal[:, s], total[:, s]))
                            if layer > 1:
                                settle(dve.tensor_tensor(rtotal[:, s], rtotal[:, s], valid[:, s], ALU.mult))
                        dve.wait_ge(context_in_psum[s], layer + 1)
                        if layer <= 1:
                            dve.wait_ge(residual_ready[s], layer + 1)
                        kept = residual if layer <= 1 else x
                        if layer == 0:
                            settle(dve.tensor_tensor(y[:, s], by_graph(B[s], D), kept[:, s], ALU.add))
                        else:
                            for g in range(G):
                                m = dve.scalar_tensor_tensor(y[:, s, g], B[s][:, g * D:(g + 1) * D],
                                                             rtotal[:, s, g:g + 1], kept[:, s, g],
                                                             ALU.mult, ALU.add)
                            settle(m)
                        for g in range(G):
                            m = dve.bn_stats(bn[:, s, g], y[:, s, g])
                        settle(m)
                        for g in range(G):
                            m = dve.bn_aggr(mv[:, s, g], bn[:, s, g])
                        m.then_inc(stats_ready[s], 1)
                    if now := item(i):
                        layer, s = now
                        dve.wait_ge(qk_in_psum[s], layer + 2)
                        if layer == 1:
                            m = dve.tensor_scalar(qT[:, s].rearrange("p k g n -> p (k g n)"), B[s][:, :],
                                                  SCALE[1], None, ALU.mult)
                        else:
                            dve.tensor_scalar(flat(qT[:, s, 0]), B[s][:, 0:G * N], col(f"bq{layer}"),
                                              SCALE[layer], ALU.add, ALU.mult)
                            m = dve.tensor_scalar(flat(kT[:, s, 0]), B[s][:, G * N:2 * G * N],
                                                  col(f"bk{layer}"), None, ALU.add)
                        m.then_inc(qk_ready[s], 1)
                    if now := normalised(i):
                        layer, s = now
                        dve.wait_ge(rough_ready[s], layer + 1)
                        settle(dve.scalar_tensor_tensor(step_a[:, s], mv[:, s, :, 1], EPS, rough[:, s],
                                                        ALU.add, ALU.mult))
                        settle(dve.tensor_tensor(step_b[:, s], step_a[:, s], rough[:, s], ALU.mult))
                        settle(dve.tensor_scalar(step_a[:, s], step_b[:, s], -0.5, 1.5, ALU.mult, ALU.add))
                        settle(dve.tensor_tensor(rstd[:, s], step_a[:, s], rough[:, s], ALU.mult))
                        dve.scalar_tensor_tensor(shift[:, s], mv[:, s, :, 0], -1.0, rstd[:, s], ALU.mult,
                                                 ALU.mult).then_inc(rstd_ready[s], 1)
                        dve.wait_ge(z_ready[s], layer + 1)
                        dve.tensor_tensor(zg[:, s], z[:, s], row_of_each(f"gamma{layer}"),
                                          ALU.mult).then_inc(zg_ready[s], 1)

        @block.gpsimd
        def _(pool):
            with pool.Fori(0, PASSES):
                pool.wait_ge(go, 1)
                pool.nop(nofuse=True)
                for s in range(S):
                    pool.tensor_tensor(residual[:, s], x0[:, s], row_of_each("bo0"),
                                       ALU.add).then_inc(residual_ready[s], 1)
                pool.wait_ge(go_cleared, 1)
                pool.nop(nofuse=True)
                for i in slots:
                    if now := normalised(i):
                        layer, s = now
                        if layer == LAYERS - 1 and s == 0:
                            pool.wait_ge(x_out_free, 1)
                        pool.wait_ge(zg_ready[s], layer + 1)
                        new = x_out if layer == LAYERS - 1 else x
                        pool.tensor_tensor(new[:, s], zg[:, s], row_of_each(f"beta{layer}"),
                                           ALU.add).then_inc(x_ready[s], 1)
                        if layer == 0:
                            pool.wait_ge(x_ready[s], 1)
                            pool.tensor_tensor(residual[:, s], x[:, s], row_of_each("bo1"),
                                               ALU.add).then_inc(residual_ready[s], 1)


def kernel(**inputs):
    import numpy as np
    import concourse.bacc as bacc
    from concourse.bass_utils import run_bass_kernel_spmd

    a = {name: np.asarray(value) for name, value in inputs.items()}
    x = a["x"].reshape(PASSES, S, G, N, D)
    rows_of = {"bv0": a["L0_gnn_bv"], "bo0": a["L0_gnn_bo"], "bo1": a["L1_gnn_bo"]}
    cols_of = {"bq0": a["L0_gnn_bq"], "bk0": a["L0_gnn_bk"]}
    weights_of = {f"w{m}0": a[f"L0_gnn_W{m}"] for m in "qkvo"}
    weights_of |= {f"w{m}T1": a[f"L1_gnn_W{m}"].T for m in "qkv"} | {"wo1": a["L1_gnn_Wo"]}
    for layer in range(2):
        rows_of[f"gamma{layer}"], rows_of[f"beta{layer}"] = a[f"L{layer}_gnn_gamma"], a[f"L{layer}_gnn_beta"]
    for layer in range(2, LAYERS):
        name, k = f"L{2 + (layer - 2) // 2}_gnn_", (layer - 2) % 2
        rows_of[f"gamma{layer}"], rows_of[f"beta{layer}"] = a[name + "ln_g"][k], a[name + "ln_b"][k]
        cols_of[f"bq{layer}"], cols_of[f"bk{layer}"] = a[name + "bq"][k], a[name + "bk"][k]
        for m in "qkc":
            weights_of[f"w{m}T{layer}"] = a[name + f"W{m}"][k].T
    arrays = {
        "x_in": x.transpose(0, 3, 1, 2, 4),
        "xT_in": x.reshape(PASSES, S, G, N, KD, P).transpose(0, 5, 1, 4, 2, 3),
        "adj_in": a["adj"].reshape(PASSES, S, G, N, N).transpose(0, 3, 1, 2, 4),
        "w_in": np.concatenate([weights_of[n].reshape(KD, P, width).transpose(1, 0, 2).reshape(P, KD * width)
                                for n, (_, width) in WEIGHTS.items()], axis=1),
        "rows_in": np.stack([rows_of[n] for n in ROWS]),
        "cols_in": np.concatenate([cols_of[n].reshape(-1, P).T for n in COLUMNS], axis=1),
        "eye_in": np.eye(P, dtype=np.float32),
    }
    arrays = {name: np.ascontiguousarray(value) for name, value in arrays.items()}
    nc = bacc.Bacc("TRN2", target_bir_lowering=False, num_devices=1)
    args = [nc.dram_tensor(name, value.shape, mybir.dt.from_np(value.dtype), kind="ExternalInput").ap()
            for name, value in arrays.items()]
    out = nc.dram_tensor("out", (PASSES, N, S, G, D), F32, kind="ExternalOutput").ap()
    gnn_stack(nc, *args, out)
    r = run_bass_kernel_spmd(nc, [arrays], core_ids=[0])
    return r.results[0]["out"].transpose(0, 2, 3, 1, 4).reshape(GRAPHS, N, D)
```

```python
from contextlib import ExitStack

import concourse.bass as bass
from concourse import mybir

F32 = mybir.dt.float32
F32R = mybir.dt.float32r
BF16 = mybir.dt.bfloat16
I32 = mybir.dt.int32
ALU = mybir.AluOpType
ACT = mybir.ActivationFunctionType
AX_X = mybir.AxisListType.X

GRAPHS, N, D = 128, 128, 256
P = 128
KD = D // P
G = 2
S = 4
PASSES = GRAPHS // (G * S)
HEADS = 8
HD = D // HEADS
QUAD = P // HD
LAYERS = 6
EPS = 1e-5
MASKED = -(2.0**100)
SCALE = [HD**-0.5, D**-0.5] + [P**-0.5] * 4

CHUNKS = [
    [("wq0", D), ("wk0", D), ("wv0", D), ("wo0", D)],
    [("wqT1", D), ("wkT1", D), ("wvT1", D), ("wo1", D)],
    [(f"{m}{layer}", width) for layer in (2, 3) for m, width in (("wqT", P), ("wkT", P), ("wcT", D))],
    [(f"{m}{layer}", width) for layer in (4, 5) for m, width in (("wqT", P), ("wkT", P), ("wcT", D))],
]
CHUNK = KD * sum(width for _, width in CHUNKS[0])
SPLIT = {}
for _name, _width in CHUNKS[0][:3] + [("scores1", D), ("values1", D)] + CHUNKS[2] + CHUNKS[3]:
    SPLIT[_name] = (sum(KD * w for _, w in SPLIT.values()), _width)
SPLIT_COLUMNS = sum(KD * width for _, width in SPLIT.values())
ROWS = ["bv0", "bo0", "bo1"] + [f"{m}{layer}" for layer in range(LAYERS) for m in ("gamma", "beta")]
COLUMNS = {"bq0": 0, "bk0": KD} | {f"{m}{layer}": 2 * KD + 2 * (layer - 2) + n
                                   for layer in range(2, LAYERS) for n, m in enumerate(("bq", "bk"))}
COLUMN_COUNT = 2 * KD + 2 * (LAYERS - 2)

CHAIN = [(layer, s) for layer in range(1, LAYERS) for s in range(S)]
ALL = [(0, s) for s in range(S)] + CHAIN
SLOTS = range(-2, len(CHAIN) + 2)
STEPS = range(HEADS * S + 2 * S)


def after_layer(layer, s):
    return layer * S + s + 1


def after_tile(layer, s, head=0):
    return (head if layer == 0 else HEADS + layer - 1) * S + s + 1


def after_chain(layer, s):
    return (layer - 1) * S + s + 1


def projected(i):
    return CHAIN[i] if 0 <= i < len(CHAIN) else None


def normalised(i):
    return ALL[i - 2 + S] if 0 <= i - 2 + S < len(ALL) else None


def head_of(j):
    return (j // S, j % S) if 0 <= j < HEADS * S else None


def gnn_stack(nc: bass.Bass, x_in, xT_in, adj_in, w_in, rows_in, cols_in, eye_in, out):
    ctx = ExitStack()

    def sb(name, shape, dtype=F32):
        return ctx.enter_context(nc.sbuf_tensor(name, [P] + shape, dtype))

    def sem(name):
        return ctx.enter_context(nc.semaphore(name))

    with ctx:
        w_hi = sb("w_hi", [SPLIT_COLUMNS], F32R)
        w_lo = sb("w_lo", [SPLIT_COLUMNS], F32R)
        wo0 = sb("wo0", [KD, D])
        rows = sb("rows", [len(ROWS), D])
        cols = sb("cols", [COLUMN_COUNT])
        eye = sb("eye", [P])
        eye16 = sb("eye16", [P], BF16)
        eps = sb("eps", [1])
        x0 = sb("x0", [S, G, D])
        x0T = sb("x0T", [S, KD, G, N])
        adj = sb("adj", [S, G, N], I32)
        x_out = sb("x_out", [S, G, D])
        mask = sb("mask", [S, G, N], BF16)
        x = sb("x", [S, G, D])
        residual = sb("residual", [S, G, D])
        xT_hi = sb("xT_hi", [S, KD, G, N], F32R)
        xT_lo = sb("xT_lo", [S, KD, G, N], F32R)
        qT = sb("qT", [S, KD, G, N])
        kT = sb("kT", [S, KD, G, N])
        v = sb("v", [S, G, D])
        probs = sb("probs", [S, G, N])
        probsT = sb("probsT", [S, G, N])
        headsT = sb("headsT", [S, HEADS // QUAD, G, N])
        y = sb("y", [S, G, D])
        z = sb("z", [S, G, D])
        negmax = sb("negmax", [S, G])
        valid = sb("valid", [S, G])
        total = sb("total", [S, G])
        rtotal = sb("rtotal", [S, G])
        bn = sb("bn", [S, G, 6])
        mv = sb("mv", [S, G, 2])
        log_var = sb("log_var", [S, G])
        rough = sb("rough", [S, G])
        step_a = sb("step_a", [S, G])
        step_b = sb("step_b", [S, G])
        rstd = sb("rstd", [S, G])
        shift = sb("shift", [S, G])

        A, B = [[ctx.enter_context(nc.psum_tensor(f"bank{b}_{s}", [P, 512], F32)) for s in range(S)] for b in "AB"]

        consts_loaded = sem("consts_loaded")
        consts_ready = sem("consts_ready")
        fused_in_psum = sem("fused_in_psum")
        scores1_ready = sem("scores1_ready")
        values1_ready = sem("values1_ready")
        w_hi_ready = sem("w_hi_ready")
        w_lo_ready = sem("w_lo_ready")
        loaded = sem("loaded")
        stored = sem("stored")
        go = [sem("go_even"), sem("go_odd")]

        in_set = []

        def pair(name):
            both = [sem(f"{name}_{parity}") for parity in ("even", "odd")]
            in_set.append(both)
            return both

        dve_step = pair("dve_step")
        mask_ready = pair("mask_ready")
        x0T_hi_ready = pair("x0T_hi_ready")
        x0T_lo_ready = pair("x0T_lo_ready")
        q0_in_psum = pair("q0_in_psum")
        k0_in_psum = pair("k0_in_psum")
        q0_ready = pair("q0_ready")
        k0_ready = pair("k0_ready")
        v_in_psum = pair("v_in_psum")
        v0_ready = pair("v0_ready")
        v_ready = pair("v_ready")
        residual_ready = pair("residual_ready")
        valid_ready = pair("valid_ready")
        headsT_in_psum = pair("headsT_in_psum")
        headsT_ready = pair("headsT_ready")
        xT_in_psum = pair("xT_in_psum")
        xT_hi_ready = pair("xT_hi_ready")
        xT_lo_ready = pair("xT_lo_ready")
        keys1_ready = pair("keys1_ready")
        qk_in_psum = pair("qk_in_psum")
        qk_ready = pair("qk_ready")
        scores_in_psum = pair("scores_in_psum")
        negmax_ready = pair("negmax_ready")
        exp_ready = pair("exp_ready")
        rtotal_ready = pair("rtotal_ready")
        probs_ready = pair("probs_ready")
        probsT_in_psum = pair("probsT_in_psum")
        probsT_ready = pair("probsT_ready")
        context_in_psum = pair("context_in_psum")
        y_ready = pair("y_ready")
        stats_ready = pair("stats_ready")
        log_ready = pair("log_ready")
        rough_ready = pair("rough_ready")
        rstd_ready = pair("rstd_ready")
        z_ready = pair("z_ready")
        zg_ready = pair("zg_ready")
        x_ready = pair("x_ready")

        def split(which, name, kd, lo=0, hi=None):
            at, width = SPLIT[name]
            return which[:, at + kd * width + lo:at + kd * width + (width if hi is None else hi)]

        def row(name):
            return rows[:, ROWS.index(name), :]

        def row_of_each(name):
            return rows[:, ROWS.index(name):ROWS.index(name) + 1, :].to_broadcast([P, G, D])

        def col(name, ft=0):
            return cols[:, COLUMNS[name] + ft:COLUMNS[name] + ft + 1]

        def by_graph(psum, width):
            return psum[:, 0:G * width].rearrange("p (g n) -> p g n", g=G)

        def flat(t):
            return t.rearrange("p g n -> p (g n)")

        def flat3(t):
            return t.rearrange("p k g n -> p (k g n)")

        def staged(chunk):
            return (y, z, x, x_out)[chunk].ap().rearrange("p s g d -> p (s g d)")

        def raw(name, kd, lo=0, hi=None):
            for chunk, members in enumerate(CHUNKS):
                at = 0
                for member, width in members:
                    if member == name:
                        return staged(chunk)[:, at + kd * width + lo:at + kd * width + (hi or width)]
                    at += KD * width

        first_columns = KD * 3 * D
        fused_at, fused_columns = SPLIT["scores1"][0], KD * 2 * D
        later_at = SPLIT["wqT2"][0]
        fused = headsT.ap().rearrange("p s q g n -> p (s q g n)")[:, 0:fused_columns]
        pieces = [
            (slice(0, first_columns), staged(0)[:, 0:first_columns]),
            (slice(later_at, later_at + CHUNK), staged(2)),
            (slice(later_at + CHUNK, later_at + 2 * CHUNK), staged(3)),
            (slice(fused_at, fused_at + fused_columns), None),
        ]

        block = ctx.enter_context(nc.Block())

        @block.sync
        def _(sp):
            for chunk in range(len(CHUNKS)):
                sp.dma_start(staged(chunk), w_in[:, chunk * CHUNK:(chunk + 1) * CHUNK]).then_inc(consts_loaded, 16)
            sp.dma_start(rows[:, :, :], rows_in.partition_broadcast(P)).then_inc(consts_loaded, 16)
            sp.dma_start(cols[:, :], cols_in).then_inc(consts_loaded, 16)
            sp.dma_start(eye[:, :], eye_in).then_inc(consts_loaded, 16)

            def load(at):
                sp.dma_start(x0T[:, :, :, :, :], xT_in[at]).then_inc(loaded, 16)
                sp.dma_start(x0[:, :, :, :], x_in[at]).then_inc(loaded, 16)
                sp.dma_start(adj[:, :, :, :], adj_in[at]).then_inc(loaded, 16)

            def start(p):
                sp.wait_ge(loaded, 48)
                sp.nop(nofuse=True)
                sp.sem_clear(loaded)
                sp.sem_inc(go[p], 1)

            load(0)
            start(0)
            with sp.Fori(0, PASSES // 2) as i:
                for p in range(2):
                    sp.wait_ge(v0_ready[p], S)
                    sp.wait_ge(k0_ready[p], S)
                    sp.wait_ge(residual_ready[p], S)
                    sp.nop(nofuse=True)
                    sp.sem_clear(go[p])
                    load(sp.snap((i * 2 + 1 + p) % PASSES))
                    for both in in_set:
                        sp.sem_clear(both[1 - p])
                    start(1 - p)
                    for s in range(S):
                        sp.wait_ge(x_ready[p], after_layer(LAYERS - 1, s))
                        sp.dma_start(out[i * 2 + p][:, s], x_out[:, s]).then_inc(stored, 16)
                    sp.wait_ge(stored, 16 * S)
                    sp.nop(nofuse=True)
                    sp.sem_clear(stored)

        @block.tensor
        def _(pe):
            pe.wait_ge(consts_ready, 1)
            for bank, left, right in ((A, "wqT1", "wkT1"), (B, "wvT1", "wo1")):
                for ft in range(KD):
                    for kd in range(KD):
                        mm = pe.matmul(bank[ft][:, 0:D], raw(left, kd, ft * P, ft * P + P), raw(right, kd),
                                       start=kd == 0, stop=kd == KD - 1)
                    mm.then_inc(fused_in_psum, 1)

            def project(psum, s, parts):
                for n, (name, lo) in enumerate(parts):
                    for kd in range(KD):
                        for w, xT in ((w_lo, xT_hi), (w_hi, xT_lo), (w_hi, xT_hi)):
                            mm = pe.matmul(psum[:, n * G * N:(n + 1) * G * N], split(w, name, kd, lo, lo + P),
                                           flat(xT[:, s, kd]), start=kd == 0 and w is w_lo,
                                           stop=kd == KD - 1 and w is w_hi and xT is xT_hi)
                return mm

            def values(psum, s, name):
                for g in range(G):
                    for kd in range(KD):
                        for w, xT in ((w_lo, xT_hi), (w_hi, xT_lo), (w_hi, xT_hi)):
                            mm = pe.matmul(psum[:, g * D:(g + 1) * D], xT[:, s, kd, g], split(w, name, kd),
                                           start=kd == 0 and w is w_lo,
                                           stop=kd == KD - 1 and w is w_hi and xT is xT_hi)
                return mm

            def masked(s):
                pe.matmul(B[s][:, 0:G * N], eye16[:, :], flat(mask[:, s]), start=True, stop=False)

            def transpose_probs(p, layer, s, head=0):
                for g in range(G):
                    t = pe.transpose(A[s][:, g * N:(g + 1) * N], probs[:, s, g], eye[:, :])
                t.then_inc(probsT_in_psum[p], 1)

            def transpose_x(p, layer, s):
                pe.wait_ge(x_ready[p], after_layer(layer - 1, s))
                for kd in range(KD):
                    for g in range(G):
                        t = pe.transpose(A[s][:, (kd * G + g) * N:(kd * G + g + 1) * N],
                                         x[:, s, g, kd * P:(kd + 1) * P], eye[:, :])
                t.then_inc(xT_in_psum[p], 1)

            def start_qk(p, s, before=None):
                pe.wait_ge(x0T_hi_ready[p], s + 1)
                pe.wait_ge(x0T_lo_ready[p], s + 1)
                project(A[s], s, [("wq0", 0), ("wq0", P)]).then_inc(q0_in_psum[p], 1)
                if before is not None:
                    pe.wait_ge(y_ready[before], after_layer(LAYERS - 1, s))
                project(B[s], s, [("wk0", 0), ("wk0", P)]).then_inc(k0_in_psum[p], 1)

            def start_v(p, s):
                pe.wait_ge(q0_ready[p], s + 1)
                values(A[s], s, "wv0").then_inc(v_in_psum[p], 1)

            pe.wait_ge(w_hi_ready, len(pieces))
            pe.wait_ge(w_lo_ready, len(pieces))
            pe.wait_ge(go[0], 1)
            pe.nop(nofuse=True)
            for s in range(S):
                start_qk(0, s)
            for s in range(S):
                start_v(0, s)

            with pe.Fori(0, PASSES // 2):
                for p in range(2):
                    for j in STEPS:
                        if now := head_of(j - 2 * S):
                            head, s = now
                            pe.wait_ge(probsT_ready[p], after_tile(0, s, head))
                            r = head % QUAD * HD
                            for g in range(G):
                                mm = pe.matmul(A[s][r:r + HD, (G + g) * N:(G + g + 1) * N],
                                               v[:, s, g, head * HD:(head + 1) * HD], probsT[:, s, g],
                                               start=True, stop=True, tile_position=(0, r))
                            if head % QUAD == QUAD - 1:
                                mm.then_inc(headsT_in_psum[p], 1)
                        if now := head_of(j):
                            head, s = now
                            if head == 0:
                                pe.wait_ge(mask_ready[p], s + 1)
                                pe.wait_ge(k0_ready[p], s + 1)
                            else:
                                pe.wait_ge(exp_ready[p], after_tile(0, s, head - 1))
                            masked(s)
                            r = head % QUAD * HD
                            for g in range(G):
                                mm = pe.matmul(B[s][:, g * N:(g + 1) * N], qT[r:r + HD, s, head // QUAD, g],
                                               kT[r:r + HD, s, head // QUAD, g], start=False, stop=g == G - 1)
                            mm.then_inc(scores_in_psum[p], 1)
                        if now := head_of(j - S):
                            head, s = now
                            if head == 0:
                                pe.wait_ge(v0_ready[p], s + 1)
                            if head == QUAD:
                                pe.wait_ge(headsT_ready[p], s + 1)
                            pe.wait_ge(probs_ready[p], after_tile(0, s, head))
                            transpose_probs(p, 0, s, head)
                    for s in range(S):
                        pe.wait_ge(headsT_ready[p], S + s + 1)
                        for g in range(G):
                            for kd in range(KD):
                                mm = pe.matmul(B[s][:, g * D:(g + 1) * D], headsT[:, s, kd, g], wo0[:, kd],
                                               start=kd == 0, stop=kd == KD - 1)
                        mm.then_inc(context_in_psum[p], 1)

                    for i in SLOTS:
                        last = i == len(CHAIN)
                        if now := projected(i - 1):
                            layer, s = now
                            pe.wait_ge(qk_ready[p], after_chain(layer, s))
                            masked(s)
                            parts = range(KD) if layer == 1 else range(1)
                            for g in range(G):
                                for kd in parts:
                                    mm = pe.matmul(B[s][:, g * N:(g + 1) * N], qT[:, s, kd, g], kT[:, s, kd, g],
                                                   start=False, stop=g == G - 1 and kd == parts[-1])
                            mm.then_inc(scores_in_psum[p], 1)
                        if now := projected(i - 2):
                            layer, s = now
                            pe.wait_ge(probsT_ready[p], after_tile(layer, s))
                            for g in range(G):
                                mm = pe.matmul(B[s][:, g * D:(g + 1) * D], probsT[:, s, g], v[:, s, g],
                                               start=True, stop=True)
                            mm.then_inc(context_in_psum[p], 1)
                        if now := projected(i):
                            layer, s = now
                            pe.wait_ge(xT_hi_ready[p], after_chain(layer, s))
                            pe.wait_ge(xT_lo_ready[p], after_chain(layer, s))
                            parts = ([("scores1", 0), ("scores1", P)] if layer == 1
                                     else [(f"wqT{layer}", 0), (f"wkT{layer}", 0)])
                            project(B[s], s, parts).then_inc(qk_in_psum[p], 1)
                        if last:
                            pe.wait_ge(go[1 - p], 1)
                            pe.nop(nofuse=True)
                            start_qk(1 - p, 0, p)
                        if now := projected(i - 1):
                            layer, s = now
                            pe.wait_ge(v_ready[p], after_chain(layer, s))
                            pe.wait_ge(exp_ready[p], after_tile(layer, s))
                            transpose_probs(p, layer, s)
                        if last:
                            start_qk(1 - p, 1, p)
                            start_v(1 - p, 0)
                        if now := projected(i + 1):
                            layer, s = now
                            transpose_x(p, layer, s)
                        if now := projected(i):
                            layer, s = now
                            name = "values1" if layer == 1 else f"wcT{layer}"
                            values(A[s], s, name).then_inc(v_in_psum[p], 1)
                    for s in range(2, S):
                        start_qk(1 - p, s, p)
                        start_v(1 - p, s - 1)
                    start_v(1 - p, S - 1)

        @block.scalar
        def _(act):
            act.preload_act_table_set("natural_log_exp_and_others")
            act.wait_ge(consts_ready, 1)
            for kd in range(KD):
                act.copy(wo0[:, kd], raw("wo0", kd))
            for at, source in pieces:
                if source is None:
                    act.wait_ge(scores1_ready, 2)
                    act.wait_ge(values1_ready, 2)
                    source = fused
                act.copy(w_hi[:, at], source).then_inc(w_hi_ready, 1)

            def softmax(p, layer, s, head=0):
                act.wait_ge(negmax_ready[p], after_tile(layer, s, head))
                if head > 0:
                    act.wait_ge(probsT_in_psum[p], after_tile(layer, s, head - 1))
                for g in range(G):
                    e = act.activation(probs[:, s, g], B[s][:, g * N:(g + 1) * N], ACT.Exp,
                                       bias=negmax[:, s, g:g + 1], accum_out=total[:, s, g:g + 1])
                e.then_inc(exp_ready[p], 1)

            def move_probsT(p, layer, s, head=0):
                act.wait_ge(probsT_in_psum[p], after_tile(layer, s, head))
                act.copy(flat(probsT[:, s]), A[s][:, 0:G * N]).then_inc(probsT_ready[p], 1)

            def split_x0T(p, s):
                act.copy(flat3(xT_hi[:, s]), flat3(x0T[:, s])).then_inc(x0T_hi_ready[p], 1)

            def move_k0(p, s):
                act.wait_ge(k0_in_psum[p], s + 1)
                for ft in range(KD):
                    m = act.activation(flat(kT[:, s, ft]), B[s][:, ft * G * N:(ft + 1) * G * N], ACT.Identity,
                                       bias=col("bk0", ft))
                m.then_inc(k0_ready[p], 1)

            act.wait_ge(go[0], 1)
            act.nop(nofuse=True)
            for s in range(S):
                split_x0T(0, s)
            for s in range(S):
                move_k0(0, s)

            with act.Fori(0, PASSES // 2):
                for p in range(2):
                    for j in STEPS:
                        if now := head_of(j):
                            head, s = now
                            softmax(p, 0, s, head)
                        if now := head_of(j - S):
                            head, s = now
                            move_probsT(p, 0, s, head)
                    for i in SLOTS:
                        if i == len(CHAIN) - 2:
                            act.wait_ge(go[1 - p], 1)
                            act.nop(nofuse=True)
                        if i >= len(CHAIN) - 2:
                            split_x0T(1 - p, i - (len(CHAIN) - 2))
                        if now := projected(i - 1):
                            layer, s = now
                            softmax(p, layer, s)
                        if i == len(CHAIN):
                            move_k0(1 - p, 0)
                        if now := projected(i - 1):
                            layer, s = now
                            move_probsT(p, layer, s)
                        if now := normalised(i):
                            layer, s = now
                            act.wait_ge(stats_ready[p], after_layer(layer, s))
                            act.activation(log_var[:, s], mv[:, s, :, 1], ACT.Ln,
                                           bias=eps[:, 0:1]).then_inc(log_ready[p], 1)
                            act.wait_ge(log_ready[p], after_layer(layer, s))
                            act.activation(rough[:, s], log_var[:, s], ACT.Exp,
                                           scale=-0.5).then_inc(rough_ready[p], 1)
                        if now := projected(i + 1):
                            layer, s = now
                            act.wait_ge(xT_in_psum[p], after_chain(layer, s))
                            act.copy(flat3(xT_hi[:, s]), A[s][:, :]).then_inc(xT_hi_ready[p], 1)
                            if layer == 1:
                                act.copy(flat3(kT[:, s]), A[s][:, :]).then_inc(keys1_ready[p], 1)
                        if i == len(CHAIN) + 1:
                            move_k0(1 - p, 1)
                        if now := normalised(i):
                            layer, s = now
                            act.wait_ge(rstd_ready[p], after_layer(layer, s))
                            for g in range(G):
                                act.activation(z[:, s, g], y[:, s, g], ACT.Identity, bias=shift[:, s, g:g + 1],
                                               scale=rstd[:, s, g:g + 1]).then_inc(z_ready[p], 1)
                        if now := projected(i):
                            layer, s = now
                            act.wait_ge(v_in_psum[p], after_layer(layer, s))
                            act.copy(flat(v[:, s]), A[s][:, :]).then_inc(v_ready[p], 1)
                    for s in range(2, S):
                        move_k0(1 - p, s)

        @block.vector
        def _(dve):
            dve.wait_ge(consts_loaded, 16 * (len(CHUNKS) + 3))
            dve.memset(eps[:, :], EPS)
            dve.tensor_copy(eye16[:, :], eye[:, :]).then_inc(consts_ready, 1)
            steps = [0]

            def settle(p, instruction):
                steps[0] += 1
                instruction.then_inc(dve_step[p], 1)
                dve.wait_ge(dve_step[p], steps[0])

            def row_max(p, layer, s, head=0):
                dve.wait_ge(scores_in_psum[p], after_tile(layer, s, head))
                dve.tensor_reduce(negmax[:, s], by_graph(B[s], N), AX_X, ALU.max,
                                  negate=True).then_inc(negmax_ready[p], 1)

            def make_mask(p, s):
                dve.tensor_scalar(mask[:, s], adj[:, s], 0.0, MASKED, ALU.is_equal,
                                  ALU.mult).then_inc(mask_ready[p], 1)

            def move_q0(p, s):
                dve.wait_ge(q0_in_psum[p], s + 1)
                for ft in range(KD):
                    m = dve.tensor_scalar(flat(qT[:, s, ft]), A[s][:, ft * G * N:(ft + 1) * G * N],
                                          col("bq0", ft), SCALE[0], ALU.add, ALU.mult)
                m.then_inc(q0_ready[p], 1)

            def move_v0(p, s):
                dve.wait_ge(v_in_psum[p], s + 1)
                dve.tensor_tensor(v[:, s], by_graph(A[s], D), row_of_each("bv0"), ALU.add).then_inc(v0_ready[p], 1)

            for kd in range(KD):
                dve.wait_ge(fused_in_psum, kd + 1)
                dve.tensor_copy(fused[:, kd * D:(kd + 1) * D], A[kd][:, 0:D]).then_inc(scores1_ready, 1)
            for kd in range(KD):
                dve.wait_ge(fused_in_psum, KD + kd + 1)
                dve.tensor_copy(fused[:, (KD + kd) * D:(KD + kd + 1) * D], B[kd][:, 0:D]).then_inc(values1_ready, 1)
            dve.wait_ge(scores1_ready, KD)
            dve.wait_ge(values1_ready, KD)
            for n, (at, source) in enumerate(pieces):
                dve.wait_ge(w_hi_ready, n + 1)
                dve.tensor_tensor(w_lo[:, at], fused if source is None else source, w_hi[:, at].bitcast(F32),
                                  ALU.subtract).then_inc(w_lo_ready, 1)

            dve.wait_ge(go[0], 1)
            dve.nop(nofuse=True)
            for s in range(S):
                make_mask(0, s)
            for s in range(S):
                move_q0(0, s)
            for s in range(S):
                move_v0(0, s)

            with dve.Fori(0, PASSES // 2):
                for p in range(2):
                    steps[0] = 0
                    for j in STEPS:
                        if (now := head_of(j - 2 * S)) and now[0] % QUAD == QUAD - 1:
                            head, s = now
                            dve.wait_ge(headsT_in_psum[p], head // QUAD * S + s + 1)
                            dve.tensor_copy(flat(headsT[:, s, head // QUAD]),
                                            A[s][:, G * N:2 * G * N]).then_inc(headsT_ready[p], 1)
                        if now := head_of(j):
                            head, s = now
                            row_max(p, 0, s, head)
                            if head == 0:
                                dve.wait_ge(negmax_ready[p], after_tile(0, s))
                                dve.tensor_scalar(valid[:, s], negmax[:, s], -0.5 * MASKED, None,
                                                  ALU.is_lt).then_inc(valid_ready[p], 1)
                        if now := head_of(j - 2):
                            head, s = now
                            dve.wait_ge(exp_ready[p], after_tile(0, s, head))
                            dve.wait_ge(valid_ready[p], s + 1)
                            settle(p, dve.tensor_tensor(rtotal[:, s], total[:, s], valid[:, s], ALU.mult))
                            settle(p, dve.reciprocal(rtotal[:, s], rtotal[:, s]))
                            for g in range(G):
                                m = dve.tensor_scalar(probs[:, s, g], probs[:, s, g], rtotal[:, s, g:g + 1], None,
                                                      ALU.mult)
                            m.then_inc(probs_ready[p], 1)
                    for i in SLOTS:
                        if i == len(CHAIN):
                            dve.wait_ge(go[1 - p], 1)
                            dve.nop(nofuse=True)
                        if now := projected(i - 1):
                            layer, s = now
                            row_max(p, layer, s)
                        if i == len(CHAIN):
                            for s in range(S):
                                make_mask(1 - p, s)
                        if now := normalised(i):
                            layer, s = now
                            if layer > 1:
                                dve.wait_ge(rtotal_ready[p], after_chain(layer, s))
                                settle(p, dve.tensor_tensor(rtotal[:, s], rtotal[:, s], valid[:, s], ALU.mult))
                            elif layer == 1:
                                dve.wait_ge(rtotal_ready[p], after_chain(layer, s))
                            dve.wait_ge(context_in_psum[p], after_layer(layer, s))
                            if layer <= 1:
                                dve.wait_ge(residual_ready[p], after_layer(layer, s))
                            kept = residual if layer <= 1 else x
                            if layer == 0:
                                dve.tensor_tensor(y[:, s], by_graph(B[s], D), kept[:, s],
                                                  ALU.add).then_inc(y_ready[p], 1)
                            else:
                                for g in range(G):
                                    m = dve.scalar_tensor_tensor(y[:, s, g], B[s][:, g * D:(g + 1) * D],
                                                                 rtotal[:, s, g:g + 1], kept[:, s, g],
                                                                 ALU.mult, ALU.add)
                                m.then_inc(y_ready[p], 1)
                            dve.wait_ge(y_ready[p], after_layer(layer, s))
                            for g in range(G):
                                m = dve.bn_stats(bn[:, s, g], y[:, s, g])
                            settle(p, m)
                            for g in range(G):
                                m = dve.bn_aggr(mv[:, s, g], bn[:, s, g])
                            m.then_inc(stats_ready[p], 1)
                        if now := projected(i):
                            layer, s = now
                            dve.wait_ge(qk_in_psum[p], after_chain(layer, s))
                            if layer == 1:
                                m = dve.tensor_scalar(flat3(qT[:, s]), B[s][:, :], SCALE[1], None, ALU.mult)
                            else:
                                dve.tensor_scalar(flat(qT[:, s, 0]), B[s][:, 0:G * N], col(f"bq{layer}"),
                                                  SCALE[layer], ALU.add, ALU.mult)
                                m = dve.tensor_scalar(flat(kT[:, s, 0]), B[s][:, G * N:2 * G * N],
                                                      col(f"bk{layer}"), None, ALU.add)
                            m.then_inc(qk_ready[p], 1)
                        if i == len(CHAIN):
                            move_q0(1 - p, 0)
                        if i == len(CHAIN) + 1:
                            move_q0(1 - p, 1)
                            move_v0(1 - p, 0)
                        if now := normalised(i):
                            layer, s = now
                            dve.wait_ge(rough_ready[p], after_layer(layer, s))
                            settle(p, dve.scalar_tensor_tensor(step_a[:, s], mv[:, s, :, 1], EPS, rough[:, s],
                                                               ALU.add, ALU.mult))
                            settle(p, dve.scalar_tensor_tensor(step_b[:, s], step_a[:, s], -0.5, rough[:, s],
                                                               ALU.mult, ALU.mult))
                            settle(p, dve.scalar_tensor_tensor(rstd[:, s], step_b[:, s], 1.5, rough[:, s],
                                                               ALU.add, ALU.mult))
                            dve.scalar_tensor_tensor(shift[:, s], mv[:, s, :, 0], -1.0, rstd[:, s], ALU.mult,
                                                     ALU.mult).then_inc(rstd_ready[p], 1)
                        if now := projected(i - 1):
                            layer, s = now
                            dve.wait_ge(exp_ready[p], after_tile(layer, s))
                            dve.reciprocal(rtotal[:, s], total[:, s]).then_inc(rtotal_ready[p], 1)
                        if now := projected(i + 1):
                            layer, s = now
                            dve.wait_ge(xT_hi_ready[p], after_chain(layer, s))
                            if layer == 1:
                                dve.wait_ge(keys1_ready[p], s + 1)
                            dve.tensor_tensor(flat3(xT_lo[:, s]), A[s][:, :], flat3(xT_hi[:, s]).bitcast(F32),
                                              ALU.subtract).then_inc(xT_lo_ready[p], 1)
                    for s in range(2, S):
                        move_q0(1 - p, s)
                        move_v0(1 - p, s - 1)
                    move_v0(1 - p, S - 1)

        @block.gpsimd
        def _(pool):
            def split_x0T(p, s):
                pool.wait_ge(x0T_hi_ready[p], s + 1)
                pool.tensor_tensor(flat3(xT_lo[:, s]), flat3(x0T[:, s]), flat3(xT_hi[:, s]).bitcast(F32),
                                   ALU.subtract).then_inc(x0T_lo_ready[p], 1)

            def make_residual0(p, s):
                pool.tensor_tensor(residual[:, s], x0[:, s], row_of_each("bo0"),
                                   ALU.add).then_inc(residual_ready[p], 1)

            pool.wait_ge(go[0], 1)
            pool.nop(nofuse=True)
            for s in range(S):
                split_x0T(0, s)
            for s in range(S):
                make_residual0(0, s)
            with pool.Fori(0, PASSES // 2):
                for p in range(2):
                    for i in SLOTS:
                        if i == len(CHAIN) - 2:
                            pool.wait_ge(go[1 - p], 1)
                            pool.nop(nofuse=True)
                        if i >= len(CHAIN) - 2:
                            split_x0T(1 - p, i - (len(CHAIN) - 2))
                        if now := normalised(i):
                            layer, s = now
                            before = after_layer(layer, s) - 1
                            new = x_out if layer == LAYERS - 1 else x
                            for g in range(G):
                                pool.wait_ge(z_ready[p], before * G + g + 1)
                                pool.tensor_tensor(z[:, s, g], z[:, s, g], row(f"gamma{layer}"),
                                                   ALU.mult).then_inc(zg_ready[p], 1)
                            for g in range(G):
                                pool.wait_ge(zg_ready[p], before * G + g + 1)
                                m = pool.tensor_tensor(new[:, s, g], z[:, s, g], row(f"beta{layer}"), ALU.add)
                            m.then_inc(x_ready[p], 1)
                            if layer == 0:
                                pool.wait_ge(x_ready[p], after_layer(layer, s))
                                pool.tensor_tensor(residual[:, s], x[:, s], row_of_each("bo1"),
                                                   ALU.add).then_inc(residual_ready[p], 1)
                    for s in range(S):
                        make_residual0(1 - p, s)


def kernel(**inputs):
    import numpy as np
    import concourse.bacc as bacc
    from concourse.bass_utils import run_bass_kernel_spmd

    a = {name: np.asarray(value) for name, value in inputs.items()}
    x = a["x"].reshape(PASSES, S, G, N, D)
    rows_of = {"bv0": a["L0_gnn_bv"], "bo0": a["L0_gnn_bo"], "bo1": a["L1_gnn_bo"]}
    cols_of = {"bq0": a["L0_gnn_bq"], "bk0": a["L0_gnn_bk"]}
    weights_of = {f"w{m}0": a[f"L0_gnn_W{m}"] for m in "qkvo"}
    weights_of |= {f"w{m}T1": a[f"L1_gnn_W{m}"].T for m in "qkv"} | {"wo1": a["L1_gnn_Wo"]}
    for layer in range(2):
        rows_of[f"gamma{layer}"], rows_of[f"beta{layer}"] = a[f"L{layer}_gnn_gamma"], a[f"L{layer}_gnn_beta"]
    for layer in range(2, LAYERS):
        name, k = f"L{2 + (layer - 2) // 2}_gnn_", (layer - 2) % 2
        rows_of[f"gamma{layer}"], rows_of[f"beta{layer}"] = a[name + "ln_g"][k], a[name + "ln_b"][k]
        cols_of[f"bq{layer}"], cols_of[f"bk{layer}"] = a[name + "bq"][k], a[name + "bk"][k]
        for m in "qkc":
            weights_of[f"w{m}T{layer}"] = a[name + f"W{m}"][k].T
    arrays = {
        "x_in": x.transpose(0, 3, 1, 2, 4),
        "xT_in": x.reshape(PASSES, S, G, N, KD, P).transpose(0, 5, 1, 4, 2, 3),
        "adj_in": a["adj"].reshape(PASSES, S, G, N, N).transpose(0, 3, 1, 2, 4),
        "w_in": np.concatenate([weights_of[n].reshape(KD, P, width).transpose(1, 0, 2).reshape(P, KD * width)
                                for chunk in CHUNKS for n, width in chunk], axis=1),
        "rows_in": np.stack([rows_of[n] for n in ROWS]),
        "cols_in": np.concatenate([cols_of[n].reshape(-1, P).T for n in COLUMNS], axis=1),
        "eye_in": np.eye(P, dtype=np.float32),
    }
    arrays = {name: np.ascontiguousarray(value) for name, value in arrays.items()}
    nc = bacc.Bacc("TRN2", target_bir_lowering=False, num_devices=1)
    args = [nc.dram_tensor(name, value.shape, mybir.dt.from_np(value.dtype), kind="ExternalInput").ap()
            for name, value in arrays.items()]
    out = nc.dram_tensor("out", (PASSES, N, S, G, D), F32, kind="ExternalOutput").ap()
    gnn_stack(nc, *args, out)
    r = run_bass_kernel_spmd(nc, [arrays], core_ids=[0])
    return r.results[0]["out"].transpose(0, 2, 3, 1, 4).reshape(GRAPHS, N, D)
```

```python
from contextlib import ExitStack

import concourse.bass as bass
from concourse import mybir

F32 = mybir.dt.float32
F32R = mybir.dt.float32r
BF16 = mybir.dt.bfloat16
I32 = mybir.dt.int32
ALU = mybir.AluOpType
ACT = mybir.ActivationFunctionType

GRAPHS, N, D = 128, 128, 256
P = 128
KD = D // P
G = 2
S = 4
PASSES = GRAPHS // (G * S)
HEADS = 8
HD = D // HEADS
QUAD = P // HD
PAIR = 2 * HD
LAYERS = 6
EPS = 1e-5
MASKED = 2.0**100
SCALE = [-(HD**-0.5), -(D**-0.5)] + [-(P**-0.5)] * 4
LARGEST = 3.0e38

CHUNKS = [
    [("wq0", D), ("wk0", D), ("wv0", D), ("wo0", D)],
    [("wqT1", D), ("wkT1", D), ("wvT1", D), ("wo1", D)],
    [(f"{m}{layer}", width) for layer in (2, 3) for m, width in (("wqT", P), ("wkT", P), ("wcT", D))],
    [(f"{m}{layer}", width) for layer in (4, 5) for m, width in (("wqT", P), ("wkT", P), ("wcT", D))],
]
CHUNK = KD * sum(width for _, width in CHUNKS[0])
SPLIT = {}
for _name, _width in CHUNKS[0][:3] + [("scores1", D), ("values1", D)] + CHUNKS[2] + CHUNKS[3]:
    SPLIT[_name] = (sum(KD * w for _, w in SPLIT.values()), _width)
SPLIT_COLUMNS = sum(KD * width for _, width in SPLIT.values())
ROWS = ["bv0", "bo0", "bo1"] + [f"{m}{layer}" for layer in range(LAYERS) for m in ("gamma", "beta")]
COLUMN_WIDTHS = {"bq0": KD, "bk0": KD, "head_scale": 2}
COLUMN_WIDTHS |= {f"{m}{layer}": 1 for layer in range(2, LAYERS) for m in ("bq", "bk")}
COLUMN_WIDTHS |= {f"{m}{layer}": KD for layer in range(LAYERS - 1) for m in ("gamma", "beta")}
COLUMNS = {name: sum(list(COLUMN_WIDTHS.values())[:n]) for n, name in enumerate(COLUMN_WIDTHS)}
COLUMN_COUNT = sum(COLUMN_WIDTHS.values())

CHAIN = [(layer, s) for layer in range(1, LAYERS) for s in range(S)]
ALL = [(0, s) for s in range(S)] + CHAIN
LAG = S + 1
TRANSPOSE_AFTER = S
VALUES_AFTER = TRANSPOSE_AFTER + 3
TILE_AT = {(h, s): h * S + s * LAG for h in range(HEADS) for s in range(S)}
TILES = sorted(TILE_AT, key=TILE_AT.get)
QK0_AT = {0: 2, 1: 3}
V0_AT = {2: 1, 6: 2, 10: 3}
RESIDUAL0_AT = {1: 0, 2: 1, 6: 2, 7: 3}
JOIN_AT = {TILE_AT[HEADS - 1, s] + VALUES_AFTER + 5: s for s in range(S)}
AFTER_JOIN = {"sum": (1, 3), "rough": (2, 3), "newton": (3, 3), "norm": (4, 3), "transpose": (8, 2),
              "move_xT": (8, 2), "split": (8, 2), "project": (11, 1), "move_qk": (11, 1), "values": (13, 1),
              "move_v": (15, 1)}
STEPS = range(max(JOIN_AT) + 1)
LATE_SLOTS = range(1, len(CHAIN) + 3)


def after_layer(layer, s):
    return layer * S + s + 1


def after_tile(layer, s, head=0):
    return TILES.index((head, s)) + 1 if layer == 0 else (HEADS + layer - 1) * S + s + 1


def after_chain(layer, s):
    return (layer - 1) * S + s + 1


def projected(i):
    return CHAIN[i] if 0 <= i < len(CHAIN) else None


def normalised(i):
    return ALL[i - 2 + S] if 0 <= i - 2 + S < len(ALL) else None


def due(what, j):
    after, streams = AFTER_JOIN[what]
    s = JOIN_AT.get(j - after, S)
    return s if s < streams else None


def after_half(half, s):
    return [tile for tile in TILES if tile[0] % QUAD == QUAD - 1].index((half * QUAD + QUAD - 1, s)) + 1


def head_of(j):
    return next((tile for tile in TILES if TILE_AT[tile] == j), None)


def gnn_stack(nc: bass.Bass, x_in, xT_in, adj_in, w_in, rows_in, cols_in, eye_in, out):
    ctx = ExitStack()

    def sb(name, shape, dtype=F32):
        return ctx.enter_context(nc.sbuf_tensor(name, [P] + shape, dtype))

    def sem(name):
        return ctx.enter_context(nc.semaphore(name))

    with ctx:
        w_hi = sb("w_hi", [SPLIT_COLUMNS], F32R)
        w_lo = sb("w_lo", [SPLIT_COLUMNS], F32R)
        wo0 = sb("wo0", [KD, D])
        rows = sb("rows", [len(ROWS), D])
        cols = sb("cols", [COLUMN_COUNT])
        eye = sb("eye", [P])
        bq0 = sb("bq0", [KD, 2])
        eps = sb("eps", [1])
        x0 = sb("x0", [S, G, D])
        x0T = sb("x0T", [S, KD, G, N])
        adj = sb("adj", [S, G, N], I32)
        x_out = sb("x_out", [S, G, D])
        mask = sb("mask", [S, G, N], BF16)
        x = sb("x", [S, G, D])
        xT_hi = sb("xT_hi", [S, KD, G, N], F32R)
        xT_lo = sb("xT_lo", [S, KD, G, N], F32R)
        qT = sb("qT", [S, KD * 2, G, N])
        kT = sb("kT", [S, KD, G, N])
        v = sb("v", [S, G, D])
        scores = sb("scores", [S, G, N])
        probs = sb("probs", [S, G, N])
        probsT = sb("probsT", [S, G, N])
        headsT = sb("headsT", [S, HEADS // QUAD, G, N])
        y = sb("y", [S, G, D])
        negmax = sb("negmax", [S, G])
        valid = sb("valid", [S, G])
        rvalid = sb("rvalid", [S, G])
        total = sb("total", [S, G])
        rtotal = sb("rtotal", [S, G])
        bn = sb("bn", [S, G, 6])
        mv = sb("mv", [S, G, 2])
        log_var = sb("log_var", [S, G])
        rough = sb("rough", [S, G])
        step_a = sb("step_a", [S, G])
        step_b = sb("step_b", [S, G])
        rstd = sb("rstd", [S, G])
        shift = sb("shift", [S, G])

        A, B = [[ctx.enter_context(nc.psum_tensor(f"bank{b}_{s}", [P, 512], F32)) for s in range(S)] for b in "AB"]

        first_loaded = sem("first_loaded")
        rest_loaded = sem("rest_loaded")
        later_loaded = sem("later_loaded")
        consts_ready = sem("consts_ready")
        fused_in_psum = sem("fused_in_psum")
        scores1_ready = sem("scores1_ready")
        values1_ready = sem("values1_ready")
        w_hi_ready = sem("w_hi_ready")
        w_lo_ready = sem("w_lo_ready")
        later_w_lo_ready = sem("later_w_lo_ready")
        bias1_added = sem("bias1_added")
        loaded = sem("loaded")
        stored = sem("stored")
        go = [sem("go_even"), sem("go_odd")]

        in_set = []

        def pair(name):
            both = [sem(f"{name}_{parity}") for parity in ("even", "odd")]
            in_set.append(both)
            return both

        dve_step = pair("dve_step")
        x0T_hi_ready = pair("x0T_hi_ready")
        x0T_lo_ready = pair("x0T_lo_ready")
        q0_in_psum = pair("q0_in_psum")
        k0_in_psum = pair("k0_in_psum")
        q0_ready = pair("q0_ready")
        k0_ready = pair("k0_ready")
        v_in_psum = pair("v_in_psum")
        v0_ready = pair("v0_ready")
        v_ready = pair("v_ready")
        residual0_ready = pair("residual0_ready")
        valid_ready = pair("valid_ready")
        headsT_in_psum = pair("headsT_in_psum")
        headsT_ready = pair("headsT_ready")
        xT_in_psum = pair("xT_in_psum")
        xT_ready = pair("xT_ready")
        xT_hi_ready = pair("xT_hi_ready")
        xT_lo_ready = pair("xT_lo_ready")
        qk_in_psum = pair("qk_in_psum")
        qk_ready = pair("qk_ready")
        scores_in_psum = pair("scores_in_psum")
        negmax_ready = pair("negmax_ready")
        exp_ready = pair("exp_ready")
        rtotal0_ready = pair("rtotal0_ready")
        probs_ready = pair("probs_ready")
        probsT_in_psum = pair("probsT_in_psum")
        probsT_ready = pair("probsT_ready")
        chain_probsT_ready = pair("chain_probsT_ready")
        context_in_psum = pair("context_in_psum")
        y_ready = pair("y_ready")
        stats_ready = pair("stats_ready")
        log_ready = pair("log_ready")
        rough_ready = pair("rough_ready")
        rstd_ready = pair("rstd_ready")
        z_ready = [pair(f"z{g}_ready") for g in range(G)]
        zg_ready = pair("zg_ready")
        x_ready = pair("x_ready")

        def split(which, name, kd, lo=0, hi=None):
            at, width = SPLIT[name]
            return which[:, at + kd * width + lo:at + kd * width + (width if hi is None else hi)]

        def row(name):
            return rows[:, ROWS.index(name), :]

        def row_of_each(name):
            return rows[:, ROWS.index(name):ROWS.index(name) + 1, :].to_broadcast([P, G, D])

        def col(name, ft=0):
            return cols[:, COLUMNS[name] + ft:COLUMNS[name] + ft + 1]

        def by_graph(psum, width):
            return psum[:, 0:G * width].rearrange("p (g n) -> p g n", g=G)

        def flat(t):
            return t.rearrange("p g n -> p (g n)")

        def flat3(t):
            return t.rearrange("p k g n -> p (k g n)")

        def staged(chunk):
            if chunk == 1:
                return qT[:, S // 2:].rearrange("p s k g n -> p (s k g n)")
            return (y, None, x, x_out)[chunk].ap().rearrange("p s g d -> p (s g d)")

        def raw(name, kd, lo=0, hi=None):
            for chunk, members in enumerate(CHUNKS):
                at = 0
                for member, width in members:
                    if member == name:
                        return staged(chunk)[:, at + kd * width + lo:at + kd * width + (hi or width)]
                    at += KD * width

        first_columns = KD * 3 * D
        fused_at, fused_columns = SPLIT["scores1"][0], KD * 2 * D
        later_at = SPLIT["wqT2"][0]
        fused = headsT.ap().rearrange("p s q g n -> p (s q g n)")[:, 0:fused_columns]
        first_piece = (slice(0, first_columns), staged(0)[:, 0:first_columns])
        fused_piece = (slice(fused_at, fused_at + fused_columns), fused)
        later_pieces = [(slice(later_at + n * CHUNK, later_at + (n + 1) * CHUNK), staged(2 + n)) for n in range(2)]

        block = ctx.enter_context(nc.Block())

        @block.sync
        def _(sp):
            def load_chunk(chunk, semaphore):
                sp.dma_start(staged(chunk), w_in[:, chunk * CHUNK:(chunk + 1) * CHUNK]).then_inc(semaphore, 16)

            sp.dma_start(cols[:, :], cols_in).then_inc(first_loaded, 16)
            load_chunk(0, first_loaded)

            def load(at):
                sp.dma_start(x0T[:, :, :, :, :], xT_in[at]).then_inc(loaded, 16)
                sp.dma_start(x0[:, :, :, :], x_in[at]).then_inc(loaded, 16)
                sp.dma_start(adj[:, :, :, :], adj_in[at]).then_inc(loaded, 16)

            def start(p):
                sp.wait_ge(loaded, 48)
                sp.nop(nofuse=True)
                sp.sem_clear(loaded)
                sp.sem_inc(go[p], 1)

            load(0)
            load_chunk(1, rest_loaded)
            sp.dma_start(rows[:, :, :], rows_in.partition_broadcast(P)).then_inc(rest_loaded, 16)
            sp.dma_start(eye[:, :], eye_in).then_inc(rest_loaded, 16)
            for chunk in range(2, len(CHUNKS)):
                load_chunk(chunk, later_loaded)
            start(0)
            sp.sem_inc(y_ready[1], G * after_layer(LAYERS - 1, S - 1))
            with sp.Fori(0, PASSES // 2) as i:
                for p in range(2):
                    sp.wait_ge(v0_ready[p], S)
                    sp.wait_ge(k0_ready[p], S)
                    sp.wait_ge(y_ready[p], G * after_layer(0, S - 1))
                    sp.nop(nofuse=True)
                    sp.sem_clear(go[p])
                    load(sp.snap((i * 2 + 1 + p) % PASSES))
                    for both in in_set:
                        sp.sem_clear(both[1 - p])
                    start(1 - p)
                    for s in range(S):
                        sp.wait_ge(x_ready[p], after_layer(LAYERS - 1, s))
                        sp.dma_start(out[i * 2 + p][:, s], x_out[:, s]).then_inc(stored, 16)
                    sp.wait_ge(stored, 16 * S)
                    sp.nop(nofuse=True)
                    sp.sem_clear(stored)

        @block.tensor
        def _(pe):
            halves = ((w_lo, xT_hi), (w_hi, xT_hi), (w_hi, xT_lo))

            def project(psum, s, parts, halves_ready=()):
                for n, (name, lo) in enumerate(parts):
                    for kd in range(KD):
                        for w, xT in halves:
                            if n == 0:
                                for half, semaphore, before in halves_ready:
                                    if xT is half:
                                        pe.wait_ge(semaphore, before + kd + 1)
                            mm = pe.matmul(psum[:, n * G * N:(n + 1) * G * N], split(w, name, kd, lo, lo + P),
                                           flat(xT[:, s, kd]), start=kd == 0 and w is w_lo,
                                           stop=kd == KD - 1 and xT is xT_lo)
                return mm

            def values(psum, s, name, g):
                for kd in range(KD):
                    for w, xT in halves:
                        mm = pe.matmul(psum[:, g * D:(g + 1) * D], xT[:, s, kd, g], split(w, name, kd),
                                       start=kd == 0 and w is w_lo, stop=kd == KD - 1 and xT is xT_lo)
                return mm

            def transpose_probs(p, layer, s, head=0):
                for g in range(G):
                    t = pe.transpose(A[s][:, g * N:(g + 1) * N], probs[:, s, g], eye[:, :])
                t.then_inc(probsT_in_psum[p], 1)

            def transpose_x(p, layer, s):
                for g in range(G):
                    pe.wait_ge(z_ready[g][p], after_layer(layer - 1, s))
                for kd in range(KD):
                    for g in range(G):
                        t = pe.transpose(A[s][:, (kd * G + g) * N:(kd * G + g + 1) * N],
                                         y[:, s, g, kd * P:(kd + 1) * P], eye[:, :])
                t.then_inc(xT_in_psum[p], 1)

            def join_heads(p, s):
                pe.wait_ge(headsT_ready[p], after_half(1, s))
                for g in range(G):
                    for kd in range(KD):
                        mm = pe.matmul(B[s][:, g * D:(g + 1) * D], headsT[:, s, kd, g], wo0[:, kd],
                                       start=kd == 0, stop=kd == KD - 1)
                mm.then_inc(context_in_psum[p], 1)

            def start_qk(p, s):
                pe.wait_ge(x0T_hi_ready[p], s + 1)
                pe.wait_ge(x0T_lo_ready[p], s + 1)
                project(A[s], s, [("wq0", 0), ("wq0", P)]).then_inc(q0_in_psum[p], 1)
                pe.wait_ge(y_ready[1 - p], G * after_layer(LAYERS - 1, s))
                project(B[s], s, [("wk0", 0), ("wk0", P)]).then_inc(k0_in_psum[p], 1)

            def start_v(p, s):
                pe.wait_ge(q0_ready[p], s + 1)
                for g in range(G):
                    mm = values(A[s], s, "wv0", g)
                mm.then_inc(v_in_psum[p], 1)

            pe.wait_ge(w_lo_ready, 1)
            pe.wait_ge(go[0], 1)
            pe.nop(nofuse=True)
            start_qk(0, 0)
            start_qk(0, 1)
            start_v(0, 0)
            pe.wait_ge(rest_loaded, 48)
            for bank, left, right in ((A, "wqT1", "wkT1"), (B, "wvT1", "wo1")):
                for ft in range(KD):
                    for kd in range(KD):
                        mm = pe.matmul(bank[S // 2 + ft][:, 0:D], raw(left, kd, ft * P, ft * P + P),
                                       raw(right, kd), start=kd == 0, stop=kd == KD - 1)
                    mm.then_inc(fused_in_psum, 1)
            pe.wait_ge(scores1_ready, KD)
            pe.wait_ge(values1_ready, KD)

            def score(p, layer, s):
                pe.wait_ge(qk_ready[p], after_chain(layer, s))
                parts = range(KD) if layer == 1 else range(1)
                for g in range(G):
                    for kd in parts:
                        mm = pe.matmul(B[s][:, g * N:(g + 1) * N], qT[:, s, kd, g], kT[:, s, kd, g],
                                       start=kd == 0, stop=kd == parts[-1])
                mm.then_inc(scores_in_psum[p], 1)

            def context(p, layer, s):
                pe.wait_ge(chain_probsT_ready[p], after_chain(layer, s))
                for g in range(G):
                    mm = pe.matmul(B[s][:, g * D:(g + 1) * D], probsT[:, s, g], v[:, s, g],
                                   start=True, stop=True)
                mm.then_inc(context_in_psum[p], 1)

            def project_qk(p, layer, s):
                parts = [("scores1", 0), ("scores1", P)] if layer == 1 else [(f"wqT{layer}", 0), (f"wkT{layer}", 0)]
                before = KD * (after_chain(layer, s) - 1)
                project(B[s], s, parts, ((xT_hi, xT_hi_ready[p], before),
                                         (xT_lo, xT_lo_ready[p], before))).then_inc(qk_in_psum[p], 1)

            def project_v(p, layer, s, g):
                mm = values(A[s], s, "values1" if layer == 1 else f"wcT{layer}", g)
                if g == G - 1:
                    mm.then_inc(v_in_psum[p], 1)

            def late_slot(p, i):
                if now := projected(i - 1):
                    score(p, *now)
                if now := projected(i - 2):
                    context(p, *now)
                if now := projected(i):
                    project_qk(p, *now)
                if i == len(CHAIN):
                    pe.wait_ge(go[1 - p], 1)
                    pe.nop(nofuse=True)
                    start_qk(1 - p, 0)
                if now := projected(i - 1):
                    pe.wait_ge(v_ready[p], after_chain(*now))
                    pe.wait_ge(exp_ready[p], after_tile(*now))
                    transpose_probs(p, *now)
                if i == len(CHAIN):
                    start_qk(1 - p, 1)
                if i == len(CHAIN) + 1:
                    start_v(1 - p, 0)
                if now := projected(i + 1):
                    transpose_x(p, *now)
                if now := projected(i):
                    for g in range(G):
                        project_v(p, *now, g)

            with pe.Fori(0, PASSES // 2):
                for p in range(2):
                    for j in STEPS:
                        if now := head_of(j - VALUES_AFTER):
                            head, s = now
                            pe.wait_ge(probsT_ready[p], after_tile(0, s, head))
                            r = head % QUAD * HD
                            for g in range(G):
                                mm = pe.matmul(A[s][r:r + HD, (G + g) * N:(G + g + 1) * N],
                                               v[:, s, g, head * HD:(head + 1) * HD], probsT[:, s, g],
                                               start=True, stop=True, tile_position=(0, r))
                            if head % QUAD == QUAD - 1:
                                mm.then_inc(headsT_in_psum[p], 1)
                        if now := head_of(j):
                            head, s = now
                            if head == 0:
                                pe.wait_ge(k0_ready[p], s + 1)
                            else:
                                pe.wait_ge(negmax_ready[p], after_tile(0, s, head - 1))
                            r = head % QUAD // 2 * PAIR
                            for g in range(G):
                                mm = pe.matmul(B[s][:, g * N:(g + 1) * N],
                                               qT[r:r + PAIR, s, head // QUAD * 2 + head % 2, g],
                                               kT[r:r + PAIR, s, head // QUAD, g], start=True, stop=True)
                            mm.then_inc(scores_in_psum[p], 1)
                        if now := head_of(j - TRANSPOSE_AFTER):
                            head, s = now
                            if head == 0:
                                pe.wait_ge(v0_ready[p], s + 1)
                            if head == QUAD:
                                pe.wait_ge(headsT_ready[p], after_half(0, s))
                            pe.wait_ge(probs_ready[p], after_tile(0, s, head))
                            transpose_probs(p, 0, s, head)
                        if j in QK0_AT:
                            start_qk(p, QK0_AT[j])
                        if j in V0_AT:
                            start_v(p, V0_AT[j])
                        if j in JOIN_AT:
                            join_heads(p, JOIN_AT[j])
                        if (s := due("project", j)) is not None:
                            pe.wait_ge(w_lo_ready, 3)
                            pe.wait_ge(later_w_lo_ready, 1)
                            project_qk(p, 1, s)
                        if (s := due("transpose", j)) is not None:
                            transpose_x(p, 1, s)
                        if (s := due("values", j)) is not None:
                            for g in range(G):
                                project_v(p, 1, s, g)
                    for i in LATE_SLOTS:
                        late_slot(p, i)

        @block.scalar
        def _(act):
            act.preload_act_table_set("natural_log_exp_and_others")

            def split_hi(piece):
                at, source = piece
                act.copy(w_hi[:, at], source).then_inc(w_hi_ready, 1)

            act.wait_ge(consts_ready, 1)
            split_hi(first_piece)
            for kd in range(KD):
                act.copy(wo0[:, kd], raw("wo0", kd))

            def softmax(p, layer, s, head=0):
                act.wait_ge(negmax_ready[p], after_tile(layer, s, head))
                if head > 0:
                    act.wait_ge(probsT_in_psum[p], after_tile(layer, s, head - 1))
                for g in range(G):
                    e = act.activation(probs[:, s, g], scores[:, s, g], ACT.Exp, scale=-1.0,
                                       bias=negmax[:, s, g:g + 1], accum_out=total[:, s, g:g + 1])
                e.then_inc(exp_ready[p], 1)


            def split_x0T(p, s):
                act.copy(flat3(xT_hi[:, s]), flat3(x0T[:, s])).then_inc(x0T_hi_ready[p], 1)

            def move_q0(p, s):
                act.wait_ge(q0_in_psum[p], s + 1)
                for ft in range(KD):
                    for parity in range(2):
                        m = act.activation(flat(qT[:, s, ft * 2 + parity]), A[s][:, ft * G * N:(ft + 1) * G * N],
                                           ACT.Identity, bias=bq0[:, ft, parity:parity + 1],
                                           scale=col("head_scale", parity))
                m.then_inc(q0_ready[p], 1)

            act.wait_ge(go[0], 1)
            act.nop(nofuse=True)
            for s in range(S):
                split_x0T(0, s)
            for s in range(2):
                move_q0(0, s)
            act.wait_ge(scores1_ready, KD)
            act.wait_ge(values1_ready, KD)
            split_hi(fused_piece)
            act.wait_ge(later_loaded, 32)
            for piece in later_pieces:
                split_hi(piece)

            def move_qk(p, layer, s):
                act.wait_ge(qk_in_psum[p], after_chain(layer, s))
                if layer == 1:
                    m = act.activation(flat3(qT[:, s, 0:KD]), B[s][:, :], ACT.Copy, scale=SCALE[1])
                else:
                    act.activation(flat(qT[:, s, 0]), B[s][:, 0:G * N], ACT.Identity,
                                   bias=col(f"bq{layer}"), scale=SCALE[layer])
                    m = act.activation(flat(kT[:, s, 0]), B[s][:, G * N:2 * G * N], ACT.Identity,
                                       bias=col(f"bk{layer}"))
                m.then_inc(qk_ready[p], 1)

            def rough_rstd(p, layer, s):
                act.wait_ge(stats_ready[p], after_layer(layer, s))
                act.activation(log_var[:, s], mv[:, s, :, 1], ACT.Ln, bias=eps[:, 0:1]).then_inc(log_ready[p], 1)
                act.wait_ge(log_ready[p], after_layer(layer, s))
                act.activation(rough[:, s], log_var[:, s], ACT.Exp, scale=-0.5).then_inc(rough_ready[p], 1)

            def move_probsT(p, layer, s):
                act.wait_ge(probsT_in_psum[p], after_tile(layer, s))
                act.copy(flat(probsT[:, s]), A[s][:, 0:G * N]).then_inc(chain_probsT_ready[p], 1)

            def move_xT(p, layer, s):
                act.wait_ge(xT_in_psum[p], after_chain(layer, s))
                for kd in range(KD):
                    act.activation(flat(kT[:, s, kd]), A[s][:, kd * G * N:(kd + 1) * G * N],
                                   ACT.Identity, bias=col(f"beta{layer - 1}", kd),
                                   scale=col(f"gamma{layer - 1}", kd)).then_inc(xT_ready[p], 1)

            def normalise_graph0(p, layer, s):
                act.wait_ge(rstd_ready[p], after_layer(layer, s))
                act.activation(y[:, s, 0], y[:, s, 0], ACT.Identity, bias=shift[:, s, 0:1],
                               scale=rstd[:, s, 0:1]).then_inc(z_ready[0][p], 1)

            def move_v(p, layer, s):
                act.wait_ge(v_in_psum[p], after_layer(layer, s))
                act.copy(flat(v[:, s]), A[s][:, :]).then_inc(v_ready[p], 1)

            def late_slot(p, i):
                if i == len(CHAIN) - 2:
                    act.wait_ge(go[1 - p], 1)
                    act.nop(nofuse=True)
                if len(CHAIN) - 2 <= i < len(CHAIN) - 2 + S:
                    split_x0T(1 - p, i - (len(CHAIN) - 2))
                if now := projected(i - 1):
                    softmax(p, *now)
                if i == len(CHAIN):
                    move_q0(1 - p, 0)
                if i - 1 in LATE_SLOTS and (now := normalised(i - 1)):
                    normalise_graph0(p, *now)
                if now := projected(i):
                    move_qk(p, *now)
                if now := projected(i + 1):
                    move_xT(p, *now)
                if now := projected(i - 1):
                    move_probsT(p, *now)
                if i == len(CHAIN) + 1:
                    move_q0(1 - p, 1)
                if now := normalised(i):
                    rough_rstd(p, *now)
                if now := projected(i):
                    move_v(p, *now)

            with act.Fori(0, PASSES // 2):
                for p in range(2):
                    for j in STEPS:
                        if now := head_of(j):
                            head, s = now
                            softmax(p, 0, s, head)
                        if j in QK0_AT:
                            move_q0(p, QK0_AT[j])
                        if (s := due("move_qk", j)) is not None:
                            move_qk(p, 1, s)
                        if (s := due("rough", j)) is not None:
                            rough_rstd(p, 0, s)
                        if (s := due("norm", j)) is not None:
                            normalise_graph0(p, 0, s)
                        if (s := due("move_xT", j)) is not None:
                            move_xT(p, 1, s)
                        if (s := due("move_v", j)) is not None:
                            move_v(p, 1, s)
                    for i in LATE_SLOTS:
                        late_slot(p, i)

        @block.vector
        def _(dve):
            dve.wait_ge(first_loaded, 32)
            for layer in range(2, LAYERS):
                dve.tensor_scalar(col(f"bq{layer}"), col(f"bq{layer}"), SCALE[layer], None, ALU.mult)
            for ft in range(KD):
                for parity in range(2):
                    dve.tensor_tensor(bq0[:, ft, parity:parity + 1], col("bq0", ft),
                                      col("head_scale", parity), ALU.mult)
            dve.memset(eps[:, :], EPS).then_inc(consts_ready, 1)
            steps = [0]

            def note(p, instruction):
                steps[0] += 1
                instruction.then_inc(dve_step[p], 1)
                return steps[0]

            def least_of_rows(s, g):
                return dve.tensor_tensor_reduce(scores[:, s, g], B[s][:, g * N:(g + 1) * N], mask[:, s, g],
                                                1.0, LARGEST, ALU.add, ALU.min, negmax[:, s, g:g + 1])

            def row_max(p, layer, s, head=0):
                dve.wait_ge(scores_in_psum[p], after_tile(layer, s, head))
                if head > 0:
                    dve.wait_ge(exp_ready[p], after_tile(layer, s, head - 1))
                for g in range(G):
                    m = least_of_rows(s, g)
                m.then_inc(negmax_ready[p], 1)

            def make_mask(p, s):
                return dve.tensor_scalar(mask[:, s], adj[:, s], 0.0, MASKED, ALU.is_equal, ALU.mult)

            def move_k0(p, s):
                dve.wait_ge(k0_in_psum[p], s + 1)
                for ft in range(KD):
                    m = dve.tensor_scalar(flat(kT[:, s, ft]), B[s][:, ft * G * N:(ft + 1) * G * N],
                                          col("bk0", ft), None, ALU.add)
                m.then_inc(k0_ready[p], 1)

            def move_v0(p, s):
                dve.wait_ge(v_in_psum[p], s + 1)
                dve.tensor_tensor(v[:, s], by_graph(A[s], D), row_of_each("bv0"), ALU.add).then_inc(v0_ready[p], 1)

            def split_weight(piece, count):
                at, source = piece
                dve.wait_ge(w_hi_ready, count)
                dve.tensor_tensor(w_lo[:, at], source, w_hi[:, at].bitcast(F32), ALU.subtract).then_inc(w_lo_ready, 1)

            split_weight(first_piece, 1)
            dve.wait_ge(go[0], 1)
            dve.nop(nofuse=True)
            for s in range(S):
                make_mask(0, s)
            move_k0(0, 0)
            move_k0(0, 1)
            dve.wait_ge(rest_loaded, 48)
            move_v0(0, 0)
            for n, (bank, ready) in enumerate(((A, scores1_ready), (B, values1_ready))):
                for kd in range(KD):
                    dve.wait_ge(fused_in_psum, n * KD + kd + 1)
                    dve.tensor_copy(fused[:, (n * KD + kd) * D:(n * KD + kd + 1) * D],
                                    bank[S // 2 + kd][:, 0:D]).then_inc(ready, 1)
            dve.wait_ge(scores1_ready, KD)
            dve.wait_ge(values1_ready, KD)
            split_weight(fused_piece, 2)
            split_weight(later_pieces[1], 4)

            def newton_a(p, layer, s):
                dve.wait_ge(rough_ready[p], after_layer(layer, s))
                note(p, dve.scalar_tensor_tensor(step_a[:, s], mv[:, s, :, 1], EPS, rough[:, s], ALU.add, ALU.mult))

            def newton_b(p, layer, s):
                note(p, dve.scalar_tensor_tensor(step_b[:, s], step_a[:, s], -0.5, rough[:, s], ALU.mult, ALU.mult))

            def newton_rstd(p, layer, s):
                note(p, dve.scalar_tensor_tensor(rstd[:, s], step_b[:, s], 1.5, rough[:, s], ALU.add, ALU.mult))

            def newton_shift(p, layer, s):
                dve.scalar_tensor_tensor(shift[:, s], mv[:, s, :, 0], -1.0, rstd[:, s], ALU.mult,
                                         ALU.mult).then_inc(rstd_ready[p], 1)

            def normalise_graph1(p, layer, s):
                dve.wait_ge(rstd_ready[p], after_layer(layer, s))
                dve.tensor_scalar(y[:, s, 1], y[:, s, 1], rstd[:, s, 1:2], shift[:, s, 1:2], ALU.mult,
                                  ALU.add).then_inc(z_ready[1][p], 1)

            def reciprocal_total(p, layer, s):
                if layer > 0:
                    dve.wait_ge(exp_ready[p], after_tile(layer, s))
                    note(p, dve.reciprocal(rtotal[:, s], total[:, s]))

            def keep_valid(p, layer, s):
                if layer > 1:
                    note(p, dve.tensor_tensor(rtotal[:, s], rtotal[:, s], valid[:, s], ALU.mult))

            def add_context(p, layer, s, g):
                if g == 0:
                    dve.wait_ge(context_in_psum[p], after_layer(layer, s))
                    if layer == 0:
                        dve.wait_ge(residual0_ready[p], s + 1)
                        dve.wait_ge(valid_ready[p], s + 1)
                    else:
                        dve.wait_ge(x_ready[p], after_layer(layer - 1, s))
                kept = x0 if layer == 0 else x
                factor = rvalid if layer == 0 else rtotal
                dve.scalar_tensor_tensor(y[:, s, g], B[s][:, g * D:(g + 1) * D], factor[:, s, g:g + 1],
                                         kept[:, s, g], ALU.mult, ALU.add).then_inc(y_ready[p], 1)

            def statistics(p, layer, s):
                for g in range(G):
                    dve.wait_ge(y_ready[p], (after_layer(layer, s) - 1) * G + g + 1)
                    last = note(p, dve.bn_stats(bn[:, s, g], y[:, s, g]))
                for g in range(G):
                    dve.wait_ge(dve_step[p], last - (G - 1) + g)
                    m = dve.bn_aggr(mv[:, s, g], bn[:, s, g])
                m.then_inc(stats_ready[p], 1)

            def split_hi(p, layer, s, kd):
                dve.wait_ge(xT_ready[p], (after_chain(layer, s) - 1) * KD + kd + 1)
                dve.tensor_copy(flat(xT_hi[:, s, kd]), flat(kT[:, s, kd])).then_inc(xT_hi_ready[p], 1)

            def split_lo(p, layer, s, kd):
                dve.wait_ge(xT_hi_ready[p], (after_chain(layer, s) - 1) * KD + kd + 1)
                dve.tensor_tensor(flat(xT_lo[:, s, kd]), flat(kT[:, s, kd]), flat(xT_hi[:, s, kd]).bitcast(F32),
                                  ALU.subtract).then_inc(xT_lo_ready[p], 1)

            def late_slot(p, i):
                if i == len(CHAIN):
                    dve.wait_ge(go[1 - p], 1)
                    dve.nop(nofuse=True)
                refined = normalised(i - 1) if i - 1 in LATE_SLOTS else None
                scored = projected(i - 1)
                summed = normalised(i)
                if scored:
                    dve.wait_ge(scores_in_psum[p], after_tile(*scored))
                    least_of_rows(scored[1], 0)
                if refined:
                    newton_a(p, *refined)
                    done = steps[0]
                if scored:
                    least_of_rows(scored[1], 1).then_inc(negmax_ready[p], 1)
                if refined:
                    dve.wait_ge(dve_step[p], done)
                    newton_b(p, *refined)
                    done = steps[0]
                if i - 1 in LATE_SLOTS and (now := projected(i)):
                    split_lo(p, *now, 1)
                if refined:
                    dve.wait_ge(dve_step[p], done)
                    newton_rstd(p, *refined)
                    done = steps[0]
                if summed:
                    reciprocal_total(p, *summed)
                    inverted = steps[0]
                if refined:
                    dve.wait_ge(dve_step[p], done)
                    newton_shift(p, *refined)
                if i == len(CHAIN):
                    dve.wait_ge(negmax_ready[p], after_tile(LAYERS - 1, S - 1))
                    for s in range(S):
                        make_mask(1 - p, s)
                if summed:
                    dve.wait_ge(dve_step[p], inverted)
                    keep_valid(p, *summed)
                    dve.wait_ge(dve_step[p], steps[0])
                    add_context(p, *summed, 0)
                if refined:
                    normalise_graph1(p, *refined)
                if summed:
                    add_context(p, *summed, 1)
                    statistics(p, *summed)
                if i == len(CHAIN):
                    move_k0(1 - p, 0)
                if i == len(CHAIN) + 1:
                    move_k0(1 - p, 1)
                    move_v0(1 - p, 0)
                if now := projected(i + 1):
                    split_hi(p, *now, 0)
                    split_hi(p, *now, 1)
                    split_lo(p, *now, 0)

            with dve.Fori(0, PASSES // 2):
                for p in range(2):
                    steps[0] = 0
                    for j in STEPS:
                        if (now := head_of(j - VALUES_AFTER)) and now[0] % QUAD == QUAD - 1:
                            head, s = now
                            dve.wait_ge(headsT_in_psum[p], after_half(head // QUAD, s))
                            dve.tensor_copy(flat(headsT[:, s, head // QUAD]),
                                            A[s][:, G * N:2 * G * N]).then_inc(headsT_ready[p], 1)
                        if now := head_of(j):
                            head, s = now
                            row_max(p, 0, s, head)
                            if head == 0:
                                dve.wait_ge(negmax_ready[p], after_tile(0, s))
                                done = note(p, dve.tensor_scalar(valid[:, s], negmax[:, s], 0.5 * MASKED, None,
                                                                 ALU.is_lt))
                                dve.wait_ge(dve_step[p], done)
                                dve.reciprocal(rvalid[:, s], valid[:, s]).then_inc(valid_ready[p], 1)
                        if now := head_of(j - TRANSPOSE_AFTER):
                            head, s = now
                            dve.wait_ge(probsT_in_psum[p], after_tile(0, s, head))
                            dve.tensor_copy(flat(probsT[:, s]), A[s][:, 0:G * N]).then_inc(probsT_ready[p], 1)
                        if now := head_of(j - 1):
                            head, s = now
                            dve.wait_ge(exp_ready[p], after_tile(0, s, head))
                            dve.reciprocal(rtotal[:, s], total[:, s]).then_inc(rtotal0_ready[p], 1)
                        if j in QK0_AT:
                            move_k0(p, QK0_AT[j])
                        if j in V0_AT:
                            move_v0(p, V0_AT[j])
                        if (s := due("sum", j)) is not None:
                            for g in range(G):
                                add_context(p, 0, s, g)
                            statistics(p, 0, s)
                        if (s := due("newton", j)) is not None:
                            for newton in (newton_a, newton_b, newton_rstd):
                                newton(p, 0, s)
                                dve.wait_ge(dve_step[p], steps[0])
                            newton_shift(p, 0, s)
                            normalise_graph1(p, 0, s)
                        if (s := due("split", j)) is not None:
                            for split_half in (split_hi, split_lo):
                                for kd in range(KD):
                                    split_half(p, 1, s, kd)
                    for i in LATE_SLOTS:
                        late_slot(p, i)

        @block.gpsimd
        def _(pool):
            def split_x0T(p, s):
                pool.wait_ge(x0T_hi_ready[p], s + 1)
                pool.tensor_tensor(flat3(xT_lo[:, s]), flat3(x0T[:, s]), flat3(xT_hi[:, s]).bitcast(F32),
                                   ALU.subtract).then_inc(x0T_lo_ready[p], 1)

            def make_residual0(p, s):
                pool.tensor_tensor(x0[:, s], x0[:, s], row_of_each("bo0"),
                                   ALU.add).then_inc(residual0_ready[p], 1)

            pool.wait_ge(go[0], 1)
            pool.nop(nofuse=True)
            for s in range(S):
                split_x0T(0, s)
            pool.wait_ge(rest_loaded, 48)
            pool.tensor_tensor(row("beta0"), row("beta0"), row("bo1"), ALU.add).then_inc(bias1_added, 1)
            pool.wait_ge(bias1_added, 1)
            at, source = later_pieces[0]
            pool.wait_ge(w_hi_ready, 3)
            pool.tensor_tensor(w_lo[:, at], source, w_hi[:, at].bitcast(F32),
                               ALU.subtract).then_inc(later_w_lo_ready, 1)

            def scale_and_shift(p, layer, s):
                before = after_layer(layer, s) - 1
                new = x_out if layer == LAYERS - 1 else x
                for g in range(G):
                    pool.wait_ge(z_ready[g][p], after_layer(layer, s))
                    pool.tensor_tensor(new[:, s, g], y[:, s, g], row(f"gamma{layer}"),
                                       ALU.mult).then_inc(zg_ready[p], 1)
                for g in range(G):
                    pool.wait_ge(zg_ready[p], before * G + g + 1)
                    m = pool.tensor_tensor(new[:, s, g], new[:, s, g], row(f"beta{layer}"), ALU.add)
                m.then_inc(x_ready[p], 1)

            def late_slot(p, i):
                if i == len(CHAIN) - 2:
                    pool.wait_ge(go[1 - p], 1)
                    pool.nop(nofuse=True)
                if len(CHAIN) - 2 <= i < len(CHAIN) - 2 + S:
                    split_x0T(1 - p, i - (len(CHAIN) - 2))
                if i - 1 in LATE_SLOTS and (now := normalised(i - 1)):
                    scale_and_shift(p, *now)

            with pool.Fori(0, PASSES // 2):
                for p in range(2):
                    for j in STEPS:
                        if now := head_of(j):
                            head, s = now
                            pool.wait_ge(rtotal0_ready[p], after_tile(0, s, head))
                            pool.tensor_tensor(probs[:, s], probs[:, s],
                                               rtotal[:, s].unsqueeze(2).to_broadcast([P, G, N]),
                                               ALU.mult).then_inc(probs_ready[p], 1)
                        if (s := due("norm", j)) is not None:
                            scale_and_shift(p, 0, s)
                        if j in RESIDUAL0_AT:
                            make_residual0(p, RESIDUAL0_AT[j])
                    for i in LATE_SLOTS:
                        late_slot(p, i)


def kernel(**inputs):
    import numpy as np
    import concourse.bacc as bacc
    from concourse.bass_utils import run_bass_kernel_spmd

    a = {name: np.asarray(value) for name, value in inputs.items()}
    x = a["x"].reshape(PASSES, S, G, N, D)
    rows_of = {"bv0": a["L0_gnn_bv"], "bo0": a["L0_gnn_bo"], "bo1": a["L1_gnn_bo"]}
    parity = np.arange(P) // HD % 2
    cols_of = {"bq0": a["L0_gnn_bq"], "bk0": a["L0_gnn_bk"],
               "head_scale": np.concatenate([SCALE[0] * (parity == n) for n in range(2)]).astype(np.float32)}
    weights_of = {f"w{m}0": a[f"L0_gnn_W{m}"] for m in "qkvo"}
    weights_of |= {f"w{m}T1": a[f"L1_gnn_W{m}"].T for m in "qkv"} | {"wo1": a["L1_gnn_Wo"]}
    for layer in range(2):
        rows_of[f"gamma{layer}"], rows_of[f"beta{layer}"] = a[f"L{layer}_gnn_gamma"], a[f"L{layer}_gnn_beta"]
    for layer in range(2, LAYERS):
        name, k = f"L{2 + (layer - 2) // 2}_gnn_", (layer - 2) % 2
        rows_of[f"gamma{layer}"], rows_of[f"beta{layer}"] = a[name + "ln_g"][k], a[name + "ln_b"][k]
        cols_of[f"bq{layer}"], cols_of[f"bk{layer}"] = a[name + "bq"][k], a[name + "bk"][k]
        for m in "qkc":
            weights_of[f"w{m}T{layer}"] = a[name + f"W{m}"][k].T
    cols_of |= {f"{m}{layer}": rows_of[f"{m}{layer}"] for layer in range(LAYERS - 1) for m in ("gamma", "beta")}
    arrays = {
        "x_in": x.transpose(0, 3, 1, 2, 4),
        "xT_in": x.reshape(PASSES, S, G, N, KD, P).transpose(0, 5, 1, 4, 2, 3),
        "adj_in": a["adj"].reshape(PASSES, S, G, N, N).transpose(0, 3, 1, 2, 4),
        "w_in": np.concatenate([weights_of[n].reshape(KD, P, width).transpose(1, 0, 2).reshape(P, KD * width)
                                for chunk in CHUNKS for n, width in chunk], axis=1),
        "rows_in": np.stack([rows_of[n] for n in ROWS]),
        "cols_in": np.concatenate([cols_of[n].reshape(-1, P).T for n in COLUMNS], axis=1),
        "eye_in": np.eye(P, dtype=np.float32),
    }
    arrays = {name: np.ascontiguousarray(value) for name, value in arrays.items()}
    nc = bacc.Bacc("TRN2", target_bir_lowering=False, num_devices=1)
    args = [nc.dram_tensor(name, value.shape, mybir.dt.from_np(value.dtype), kind="ExternalInput").ap()
            for name, value in arrays.items()]
    out = nc.dram_tensor("out", (PASSES, N, S, G, D), F32, kind="ExternalOutput").ap()
    gnn_stack(nc, *args, out)
    r = run_bass_kernel_spmd(nc, [arrays], core_ids=[0])
    return r.results[0]["out"].transpose(0, 2, 3, 1, 4).reshape(GRAPHS, N, D)
```
